# Optimizing a Trainium2 kernel written in Bass

```python
import numpy as np
import jax
import jax.numpy as jnp

def _softmax(x, axis=-1):
    return jax.nn.softmax(x, axis=axis)

def _gelu(x):
    return jax.nn.gelu(x, approximate=True)

def _silu(x):
    return jax.nn.silu(x)

def _sigmoid(x):
    return jax.nn.sigmoid(x)

def _layernorm(x, axis=-1, eps=1e-05):
    m = jnp.mean(x, axis=axis, keepdims=True)
    v = jnp.var(x, axis=axis, keepdims=True)
    return (x - m) / jnp.sqrt(v + eps)

def _scatter_add(tgt, idx, src, axis=0):
    return tgt.at[idx].add(src)

def _segment_sum(src, seg, n):
    return jax.ops.segment_sum(src, seg, n)
kernel_name = 'mk_macaron_d1_jaxref_r8_f296b4'

def setup_inputs(seed: int=0):
    np.random.seed(seed)
    _w = jnp.asarray

    def _L0_attn_setup():
        import jax, jax.numpy as jnp
        import numpy as np
        B, S, D = (4, 512, 128)
        H, HD = (16, 64)
        EPS = 1e-06

        def _feature_map(t):
            return jax.nn.elu(t) + 1.0
        key = jax.random.key(seed)
        ks = jax.random.split(key, 9)
        sd = 1.0 / np.sqrt(D)
        x = jax.random.normal(ks[0], (B, S, D), dtype=jnp.float32)
        wq = jax.random.normal(ks[1], (D, H, HD), dtype=jnp.float32) * sd
        bq = jnp.zeros((H, HD), dtype=jnp.float32)
        wk = jax.random.normal(ks[2], (D, H, HD), dtype=jnp.float32) * sd
        bk = jnp.zeros((H, HD), dtype=jnp.float32)
        wv = jax.random.normal(ks[3], (D, H, HD), dtype=jnp.float32) * sd
        bv = jnp.zeros((H, HD), dtype=jnp.float32)
        wo = jax.random.normal(ks[4], (H, HD, D), dtype=jnp.float32) * (1.0 / np.sqrt(H * HD))
        bo = jnp.zeros((D,), dtype=jnp.float32)
        return {'x': x, 'wq': wq, 'bq': bq, 'wk': wk, 'bk': bk, 'wv': wv, 'bv': bv, 'wo': wo, 'bo': bo}
    _L0_attn_in = _L0_attn_setup()

    def _L0_ffn_setup():
        import jax, jax.numpy as jnp
        import numpy as np
        TOP_K = 2
        TEMP = 0.9
        EPS = 1e-05
        B, S, D, F, E = (2, 256, 128, 512, 8)

        def _moe_forward(x, gate_w, gate_b, w1, b1, w2, b2, ln_g, ln_b):
            logits = (x @ gate_w + gate_b) / TEMP
            topk_vals, topk_idx = jax.lax.top_k(logits, TOP_K)
            keep = jax.nn.one_hot(topk_idx, E, dtype=jnp.bool_).any(-2)
            masked = jnp.where(keep, logits, -jnp.inf)
            gate_probs = jax.nn.softmax(masked, axis=-1)
            h = jnp.einsum('bsd,edf->bsef', x, w1) + b1
            h = jax.nn.gelu(h, approximate=False)
            expert_out = jnp.einsum('bsef,efd->bsed', h, w2) + b2
            out = jnp.einsum('bse,bsed->bsd', gate_probs, expert_out)
            mu = out.mean(-1, keepdims=True)
            var = out.var(-1, keepdims=True)
            out = (out - mu) / jnp.sqrt(var + EPS) * ln_g + ln_b
            return out
        key = jax.random.key(seed)
        ks = jax.random.split(key, 4)
        scale_in = 1.0 / np.sqrt(D)
        scale_ff = 1.0 / np.sqrt(F)
        return {'x': jax.random.normal(ks[0], (B, S, D), jnp.float32), 'gate_w': jax.random.normal(ks[1], (D, E), jnp.float32) * scale_in, 'gate_b': jnp.zeros((E,), jnp.float32), 'w1': jax.random.normal(ks[2], (E, D, F), jnp.float32) * scale_in, 'b1': jnp.zeros((E, F), jnp.float32), 'w2': jax.random.normal(ks[3], (E, F, D), jnp.float32) * scale_ff, 'b2': jnp.zeros((E, D), jnp.float32), 'ln_g': jnp.ones((D,), jnp.float32), 'ln_b': jnp.zeros((D,), jnp.float32)}
    _L0_ffn_in = _L0_ffn_setup()
    _d = {'L0_attn_x': _L0_attn_in['x'], 'L0_attn_wq': _L0_attn_in['wq'], 'L0_attn_bq': _L0_attn_in['bq'], 'L0_attn_wk': _L0_attn_in['wk'], 'L0_attn_bk': _L0_attn_in['bk'], 'L0_attn_wv': _L0_attn_in['wv'], 'L0_attn_bv': _L0_attn_in['bv'], 'L0_attn_wo': _L0_attn_in['wo'], 'L0_attn_bo': _L0_attn_in['bo'], 'L0_ffn_gate_w': _L0_ffn_in['gate_w'], 'L0_ffn_gate_b': _L0_ffn_in['gate_b'], 'L0_ffn_w1': _L0_ffn_in['w1'], 'L0_ffn_b1': _L0_ffn_in['b1'], 'L0_ffn_w2': _L0_ffn_in['w2'], 'L0_ffn_b2': _L0_ffn_in['b2'], 'L0_ffn_ln_g': _L0_ffn_in['ln_g'], 'L0_ffn_ln_b': _L0_ffn_in['ln_b']}
    _x0 = _d['L0_attn_x']
    _d['L0_attn_x'] = jax.random.normal(jax.random.fold_in(jax.random.key(seed), 1), (4, 512, 128), dtype=_x0.dtype)
    del _x0
    return _d

def reference(L0_attn_x, L0_attn_wq, L0_attn_bq, L0_attn_wk, L0_attn_bk, L0_attn_wv, L0_attn_bv, L0_attn_wo, L0_attn_bo, L0_ffn_gate_w, L0_ffn_gate_b, L0_ffn_w1, L0_ffn_b1, L0_ffn_w2, L0_ffn_b2, L0_ffn_ln_g, L0_ffn_ln_b):

    def _L0_attn_ref(x, wq, bq, wk, bk, wv, bv, wo, bo):
        import jax, jax.numpy as jnp
        import numpy as np
        B, S, D = (4, 512, 128)
        H, HD = (16, 64)
        EPS = 1e-06

        def _feature_map(t):
            return jax.nn.elu(t) + 1.0
        q = jnp.einsum('nsf,fhd->nshd', x, wq) + bq
        k = jnp.einsum('nsf,fhd->nshd', x, wk) + bk
        v = jnp.einsum('nsf,fhd->nshd', x, wv) + bv
        qm = _feature_map(q)
        km = _feature_map(k)
        kv = jnp.einsum('nshd,nshm->nhmd', km, v)
        z = 1.0 / (jnp.einsum('nlhd,nhd->nlh', qm, jnp.sum(km, axis=1)) + EPS)
        y = jnp.einsum('nlhd,nhmd,nlh->nlhm', qm, kv, z)
        out = jnp.einsum('nlhm,hmf->nlf', y, wo) + bo
        return out

    def _L0_ffn_ref(x, gate_w, gate_b, w1, b1, w2, b2, ln_g, ln_b):
        import jax, jax.numpy as jnp
        import numpy as np
        TOP_K = 2
        TEMP = 0.9
        EPS = 1e-05
        B, S, D, F, E = (2, 256, 128, 512, 8)

        def _moe_forward(x, gate_w, gate_b, w1, b1, w2, b2, ln_g, ln_b):
            logits = (x @ gate_w + gate_b) / TEMP
            topk_vals, topk_idx = jax.lax.top_k(logits, TOP_K)
            keep = jax.nn.one_hot(topk_idx, E, dtype=jnp.bool_).any(-2)
            masked = jnp.where(keep, logits, -jnp.inf)
            gate_probs = jax.nn.softmax(masked, axis=-1)
            h = jnp.einsum('bsd,edf->bsef', x, w1) + b1
            h = jax.nn.gelu(h, approximate=False)
            expert_out = jnp.einsum('bsef,efd->bsed', h, w2) + b2
            out = jnp.einsum('bse,bsed->bsd', gate_probs, expert_out)
            mu = out.mean(-1, keepdims=True)
            var = out.var(-1, keepdims=True)
            out = (out - mu) / jnp.sqrt(var + EPS) * ln_g + ln_b
            return out
        return _moe_forward(x, gate_w, gate_b, w1, b1, w2, b2, ln_g, ln_b)
    x = L0_attn_x
    x = x + 0.5 * _L0_ffn_ref(_layernorm(x, axis=-1), L0_ffn_gate_w, L0_ffn_gate_b, L0_ffn_w1, L0_ffn_b1, L0_ffn_w2, L0_ffn_b2, L0_ffn_ln_g, L0_ffn_ln_b)
    x = x + _L0_attn_ref(_layernorm(x, axis=-1), L0_attn_wq, L0_attn_bq, L0_attn_wk, L0_attn_bk, L0_attn_wv, L0_attn_bv, L0_attn_wo, L0_attn_bo)
    x = x + 0.5 * _L0_ffn_ref(_layernorm(x, axis=-1), L0_ffn_gate_w, L0_ffn_gate_b, L0_ffn_w1, L0_ffn_b1, L0_ffn_w2, L0_ffn_b2, L0_ffn_ln_g, L0_ffn_ln_b)
    return x

_drawn_inputs = setup_inputs


def setup_inputs(seed=0):
    import zlib

    import numpy as np

    out = dict(_drawn_inputs(seed))
    spreads = {'L0_attn_bq': (0.0, 0.8),
     'L0_attn_bk': (0.0, 0.8),
     'L0_attn_bv': (0.0, 0.1),
     'L0_attn_bo': (0.0, 0.1),
     'L0_ffn_gate_b': (0.0, 0.1),
     'L0_ffn_b1': (0.0, 0.1),
     'L0_ffn_b2': (0.0, 0.1),
     'L0_ffn_ln_g': (1.0, 0.2),
     'L0_ffn_ln_b': (0.0, 0.1)}
    factors = {'L0_attn_wq': 2.949, 'L0_attn_wk': 2.846}
    for name, (base, spread) in spreads.items():
        noise = np.random.default_rng([zlib.crc32(name.encode()), seed]).standard_normal(out[name].shape)
        drawn = base * np.exp(spread * noise) if base else spread * noise
        out[name] = jnp.asarray(drawn.astype(out[name].dtype))
    for name, factor in factors.items():
        out[name] = (out[name] * factor).astype(out[name].dtype)
    return out
```

```python
from contextlib import ExitStack

import concourse.bass as bass
from concourse import mybir

ALU = mybir.AluOpType
ACT = mybir.ActivationFunctionType
F32 = mybir.dt.float32
F32R = mybir.dt.float32r
AX_X = mybir.AxisListType.X

P = 128
TILES = 16
TB = 8
BLK = TB * P
BANK = 512
E = 8
HC = 4
HP = 8
NB = 4
ST = 4
WU = 11
TEMP = 0.9
LN_EPS = 1e-5
ATT_EPS = 1e-6
FAR = -3.0e38
FFN1, ATT, FFN2 = 0, 1, 2


def timeline():
    t = []

    def norm(r, b):
        t.extend([("stats", r, b), ("norm", r, b)])

    def gate(r, b):
        t.extend([("gate", r, b), ("probs", r, b), ("probsT", r, b)])

    def ffn(r, b, between):
        for s in range(E * HC):
            t.append(("up", r, b, s))
            t.extend(between.get(s, ()))
            if s > 0:
                t.append(("down", r, b, s - 1))
            elif b == 1:
                t.append(("down", r, 0, E * HC - 1))

    def kv_steps(n, i):
        t.extend([("K", n, i), ("V", n, i), ("Kf", n, i)])
        if i:
            t.append(("kv", n, i - 1))

    def head(n):
        kv_steps(n, 0)
        kv_steps(n, 1)

    def middle(n):
        kv_steps(n, 2)
        kv_steps(n, 3)
        t.extend([("Q", n, 0), ("kv", n, 3), ("kvout", n), ("Q", n, 1), ("Qf", n, 0), ("Q", n, 2), ("Qf", n, 1),
                  ("kvT", n), ("Q", n, 3), ("Qf", n, 2), ("Qf", n, 3), ("G", n), ("den", n)])

    def tail(n):
        t.extend([("z", n, 0), ("z", n, 1), ("out", n, 0), ("z", n, 2), ("out", n, 1), ("z", n, 3),
                  ("out", n, 2), ("out", n, 3), ("outc", n)])

    t += [("W", 0), ("W", 1)]
    t += [("stats", FFN1, 0), ("bias",), ("norm", FFN1, 0), ("xT", FFN1, 0, "C"), ("gate", FFN1, 0), ("probs", FFN1, 0)]
    between = {4 * e: [("W", e + 2)] for e in range(E)}
    between[0] += [("probsT", FFN1, 0)]
    between[24] += [("W", 10)]
    between[5] = [("stats", FFN1, 1)]
    between[6] = [("norm", FFN1, 1), ("xT", FFN1, 1, "C")]
    between[9] = [("gate", FFN1, 1)]
    between[10] = [("probs", FFN1, 1)]
    between[11] = [("probsT", FFN1, 1)]
    ffn(FFN1, 0, between)

    ffn(FFN1, 1, {4: [("accT", FFN1, 0, "C")], 6: [("addin", FFN1, 0)], 8: [("stats", ATT, 0)],
                  10: [("norm", ATT, 0), ("xT", ATT, 0, "C")]})
    t.append(("down", FFN1, 1, E * HC - 1))
    t.append(("attention",))
    head(0)
    t += [("accT", FFN1, 1, "A")]
    middle(0)
    t += [("addin", FFN1, 1)]
    head(1)
    t += [("denz", 0)]
    tail(0)
    t += [("stats", ATT, 1), ("norm", ATT, 1)]
    middle(1)
    t += [("oT", 0), ("xT", ATT, 1, "A")]
    head(2)
    t += [("denz", 1)]
    tail(1)
    middle(2)
    t += [("oT", 1), ("stats", FFN2, 0)]
    head(3)
    t += [("denz", 2), ("norm", FFN2, 0)]
    tail(2)
    t += [("xT", FFN2, 0, "A")]
    middle(3)
    t += [("oT", 2), ("denz", 3)]
    tail(3)
    t += [("oT", 3), ("ffn2",), ("gate", FFN2, 0), ("probs", FFN2, 0)]
    ffn(FFN2, 0, {0: [("probsT", FFN2, 0)], 2: [("stats", FFN2, 1)], 4: [("norm", FFN2, 1), ("xT", FFN2, 1, "C")],
                  7: [("gate", FFN2, 1)], 8: [("probs", FFN2, 1)], 9: [("probsT", FFN2, 1)]})
    ffn(FFN2, 1, {4: [("accT", FFN2, 0, "C")], 6: [("addin", FFN2, 0)]})
    t += [("down", FFN2, 1, E * HC - 1), ("accT", FFN2, 1, "C"), ("addin", FFN2, 1)]
    return t


def bass_macaron_kernel(nc: bass.Bass, x_in, wq, bq, wk, bk, wv, bv, wo, bo, gate_w, gate_b,
                        w1, b1, w2, b2, ln_g, ln_b, out):
    steps = timeline()

    place, ring_use, uses, kinds = {}, {}, {"A": 0, "C": 0}, {}
    feature_use = {}
    for st in steps:
        k = st[0]
        place[st] = kinds.get(k, 0)
        kinds[k] = place[st] + 1
        ring = st[-1] if st[-1] in ("A", "C") else (
            "A" if k in ("up", "K", "V", "Q", "kvT", "G", "z", "oT") else "C" if k in ("bias", "gate", "probsT") else None)
        if ring:
            ring_use[st] = (ring, uses[ring])
            uses[ring] += 1
        if k in ("K", "Q"):
            feature_use[st] = len(feature_use)
    assert set(place) == set(steps) and len(place) == len(steps)
    at = {st: i for i, st in enumerate(steps)}
    c_uses_before_attention = sum(1 for st, (r, _) in ring_use.items() if r == "C" and at[st] < at[("attention",)])

    ctx = ExitStack()
    with ctx:
        def sb(name, shape, dt=F32, scope=ctx):
            return scope.enter_context(nc.sbuf_tensor(name, shape, dt))

        def sem(name):
            return ctx.enter_context(nc.semaphore(name))

        x = sb("x", [P, TILES, P])
        xh = sb("xh", [P, 2, BLK], F32R)
        xl = sb("xl", [P, 2, BLK], F32R)
        Wh = sb("Wh", [P, E, 2, BANK], F32R)
        Wl = sb("Wl", [P, E, 2, BANK], F32R)
        Ah = sb("Ah", [P, 3, 2 * BANK], F32R)
        Al = sb("Al", [P, 3, 2 * BANK], F32R)
        wo_sb = sb("wo_sb", [P, HP, P])
        bkv = sb("bkv", [P, 2, 2 * BANK])
        acc = sb("acc", [P, 2, BLK])
        vt = sb("vt", [P, 2, HP, P + 1])
        kvd = sb("kvd", [P, HP, P])
        ksum = sb("ksum", [P, HP * 16])
        tok = sb("tok", [P, TB, P])
        ident = sb("ident", [P, P])
        pick = sb("pick", [48, HP, P], F32R)
        gain = sb("gain", [P, P])
        shift = sb("shift", [P, P])
        rows = sb("rows", [49, P])
        cols = sb("cols", [P, 49])
        gw = sb("gw", [P, E])
        gwh = sb("gwh", [P, E], F32R)
        gwl = sb("gwl", [P, E], F32R)
        gb = sb("gb", [P, E])
        order = sb("order", [P, E])
        half = sb("half", [P, TB])
        bst = sb("bst", [P, TB, 6])
        mv = sb("mv", [P, TB, 2])
        ve = sb("ve", [P, TB])
        rstd = sb("rstd", [P, TB])
        gL = sb("gL", [P, TB, E])
        gA = sb("gA", [P, TB, E])
        gB = sb("gB", [P, TB, E])
        gS = sb("gS", [P, TB, E])
        gX = sb("gX", [P, TB, E])
        gm1 = sb("gm1", [P, TB])
        gm2 = sb("gm2", [P, TB])
        gsum = sb("gsum", [P, TB])
        probs = sb("probs", [P, E, TB])
        pT = sb("pT", [E * TB, P])

        ffn_only = ExitStack()
        pb = sb("pb", [P, 2, BLK], scope=ffn_only)
        hid = sb("hid", [P, 2, BLK], scope=ffn_only)
        hh = sb("hh", [P, 2, BLK], F32R, scope=ffn_only)
        hl = sb("hl", [P, 2, BLK], F32R, scope=ffn_only)
        gated = sb("gated", [P, 2, BLK], scope=ffn_only)
        stage = sb("stage", [P, 2, 2, BANK], scope=ffn_only)
        ffn_only.close()
        kvTs = sb("kvTs", [P, HP, P])
        Gs = sb("Gs", [P, HP, P])
        R = sb("R", [P, 2, 2 * BANK])
        X = sb("X", [P, 2, 2 * BANK])
        km = sb("km", [P, 2, 2 * BANK])
        qm = sb("qm", [P, HP, BANK])
        z2 = sb("z2", [48, BANK], F32R)
        oT = acc[:, 0, 0:BANK]
        zr = oT[0:16, :]

        psA = ctx.enter_context(nc.psum_tensor("psA", [P, 2, 2 * BANK], F32))
        psB = ctx.enter_context(nc.psum_tensor("psB", [P, 2, BANK], F32))
        psC = ctx.enter_context(nc.psum_tensor("psC", [P, 2, BANK], F32))

        table = nc.dram_tensor("gate_table", [4, E * TB, P], F32, kind="Internal").ap()

        def ps(st):
            ring, n = ring_use[st]
            return psA[:, n % 2, :] if ring == "A" else psC[:, :, :].rearrange("p a n -> p (a n)")

        def kv_ps(c):
            t = psB[:, c // 3, :] if c < 6 else psC[:, 0, :]
            return t[:, (c % 3) * (P + 1):(c % 3 + 1) * (P + 1)]

        x_loaded = [sem("x_loaded0"), sem("x_loaded1")]
        small_loaded = sem("small_loaded")
        ln_loaded = sem("ln_loaded")
        rows_loaded = sem("rows_loaded")
        att_loaded = sem("att_loaded")
        stage_loaded = [sem("stage_loaded0"), sem("stage_loaded1")]
        table_stored = sem("table_stored")
        pb_loaded = [sem("pb_loaded0"), sem("pb_loaded1")]
        stored = sem("stored")
        consts_ready = sem("consts_ready")
        hi_split = sem("hi_split")
        w_ready = sem("w_ready")
        gw_ready = sem("gw_ready")
        cols_ready = sem("cols_ready")
        full = {"A": sem("fullA"), "C": sem("fullC")}
        b_full = sem("b_full")
        b_free = sem("b_free")
        stats_ready = sem("stats_ready")
        rstd_ready = sem("rstd_ready")
        tok_ready = sem("tok_ready")
        x_shifted = sem("x_shifted")
        xh_ready = sem("xh_ready")
        xT_ready = sem("xT_ready")
        logits_ready = sem("logits_ready")
        exp_ready = sem("exp_ready")
        probs_ready = sem("probs_ready")
        pT_ready = sem("pT_ready")
        hid_ready = sem("hid_ready")
        hl_ready = sem("hl_ready")
        down_done = sem("down_done")
        gated_ready = sem("gated_ready")
        acc_added = sem("acc_added")
        acc_in_tok = sem("acc_in_tok")
        x_ready = sem("x_ready")
        R_ready = sem("R_ready")
        X_ready = sem("X_ready")
        feature_ready = sem("feature_ready")
        v_ready = sem("v_ready")
        kv_done = sem("kv_done")
        kvd_ready = sem("kvd_ready")
        kvT_ready = sem("kvT_ready")
        G_ready = sem("G_ready")
        den_full = sem("den_full")
        den_read = sem("den_read")
        z_ready = sem("z_ready")
        qz_ready = sem("qz_ready")
        out_done = sem("out_done")
        oT_ready = sem("oT_ready")
        dve_chain = sem("dve_chain")
        pool_chain = sem("pool_chain")

        def wait_full(eng, st):
            ring, n = ring_use[st]
            eng.wait_ge(full[ring], n + 1)

        def wait_left(eng, st):
            kind, a = st[0], st[1:]
            done, n = {
                "bias": (cols_ready, 1),
                "xT": (xT_ready, place[st] + 1),
                "gate": (logits_ready, place[st] + 1),
                "probsT": (pT_ready, place[st] + 1),
                "up": (hid_ready, place[st] + 1),
                "accT": (acc_in_tok, place[st] + 1),
                "K": (R_ready, place[st] + 1),
                "V": (v_ready, place[st] + 1),
                "Q": (X_ready, feature_use.get(st, 0) + 1),
                "kvT": (kvT_ready, place[st] + 1),
                "G": (G_ready, place[st] + 1),
                "z": (qz_ready, place[st] + 1),
                "oT": (x_ready, x_writes.get(st, 0)),
            }[kind]
            eng.wait_ge(done, n)

        def wait_free(eng, st):
            ring, n = ring_use[st]
            slots = 2 if ring == "A" else 1
            if n >= slots:
                wait_left(eng, used_by[ring, n - slots])

        def expert_no(r, b, e):
            return (2 * (r == FFN2) + b) * E + e

        def blocks_before(r, b):
            return 2 * (r == FFN2) + b

        def x_parts(r, b):
            return {FFN1: None, ATT: ("addin", FFN1, b), FFN2: ("oT", 2 * b + 1)}[r]

        x_writes = {}
        for st in steps:
            if st[0] in ("addin", "oT"):
                x_writes[st] = len(x_writes) + 1
        tok_writes = {}
        for st in steps:
            if st[0] == "norm":
                tok_writes[st] = sum(k[0] == "norm" for k in tok_writes) + 1

        used_by = {v: st for st, v in ring_use.items()}
        last_c = used_by["C", c_uses_before_attention - 1]

        block = ctx.enter_context(nc.Block())

        @block.sync
        def _(sp):
            x_v = x_in.rearrange("n (t p) d -> p (n t) d", p=P)
            out_v = out.rearrange("n (t p) d -> p (n t) d", p=P)
            w2_v = w2.rearrange("e (c k) d -> e k c d", k=P)
            att_w = [w.rearrange("d h m -> d (h m)") for w in (wq, wk, wv)]
            sp.dma_start(x[:, 0:TB, :], x_v[:, 0:TB, :]).then_inc(x_loaded[0], 16)
            sp.dma_start(gw[:, :], gate_w).then_inc(small_loaded, 16)
            sp.dma_start(gb[:, :], gate_b.partition_broadcast(P)).then_inc(small_loaded, 16)
            sp.dma_start(rows[0:32, :], b1.rearrange("e (c k) -> (e c) k", k=P)).then_inc(rows_loaded, 16)
            sp.dma_start(rows[32:40, :], b2).then_inc(rows_loaded, 16)
            sp.dma_start(rows[40:48, :], bq.rearrange("(c j) m -> c (j m)", j=2)).then_inc(rows_loaded, 16)
            sp.dma_start(rows[48:49, :], bo.rearrange("(a d) -> a d", a=1)).then_inc(rows_loaded, 16)
            for st in steps:
                kind, a = st[0], st[1:]
                if kind == "W":
                    u, = a
                    if u >= 2:
                        sp.wait_ge(w_ready, u - 1)
                    s = stage[:, u % 2, :, :]
                    if u < E:
                        sp.dma_start(s[:, 0, :], w1[u]).then_inc(stage_loaded[u % 2], 16)
                        sp.dma_start(s[:, 1, :].rearrange("k (c d) -> k c d", c=HC), w2_v[u]).then_inc(stage_loaded[u % 2], 16)
                    else:
                        sp.dma_start(s.rearrange("p a n -> p (a n)"), att_w[u - E]).then_inc(stage_loaded[u % 2], 32)
                    if u == 1:
                        sp.dma_start(x[:, TB:TILES, :], x_v[:, TB:TILES, :]).then_inc(x_loaded[1], 16)
                        sp.dma_start(gain[:, :], ln_g.partition_broadcast(P)).then_inc(ln_loaded, 16)
                        sp.dma_start(shift[:, :], ln_b.partition_broadcast(P)).then_inc(ln_loaded, 16)
                    if u == 8:
                        sp.dma_start(wo_sb[:, :, :], wo.rearrange("(c j) m d -> (j m) c d", j=2)).then_inc(att_loaded, 16)
                        sp.dma_start(bkv[:, 0, :], bk.rearrange("h m -> (h m)").partition_broadcast(P)).then_inc(att_loaded, 16)
                        sp.dma_start(bkv[:, 1, :], bv.rearrange("h m -> (h m)").partition_broadcast(P)).then_inc(att_loaded, 16)
                elif kind == "probsT":
                    n = place[st]
                    sp.wait_ge(pT_ready, n + 1)
                    sp.dma_start(table[n], pT[:, :]).then_inc(table_stored, 16)
                elif kind == "down" and a[2] % HC == 0:
                    r, b, s = a
                    e = s // HC
                    g = expert_no(r, b, e)
                    sp.wait_ge(table_stored, 16 * (blocks_before(r, b) + 1))
                    if g >= 2:
                        sp.wait_ge(b_free, 2 * (g - 1))
                    row = table[blocks_before(r, b), e * TB:(e + 1) * TB, :].rearrange("t p -> (t p)")
                    sp.dma_start(pb[:, g % 2, :], row.partition_broadcast(P)).then_inc(pb_loaded[g % 2], 16)
                elif kind == "ffn2":
                    sp.wait_ge(out_done, NB)
                elif kind == "addin" and a[0] == FFN2:
                    b = a[1]
                    sp.wait_ge(x_ready, x_writes[st])
                    sp.dma_start(out_v[:, b * TB:(b + 1) * TB, :], x[:, b * TB:(b + 1) * TB, :]).then_inc(stored, 16)
            sp.wait_ge(stored, 32)

        @block.tensor
        def _(pe):
            def split3(o, ah, al, bh, bl, start, stop):
                nc.tensor.matmul(o, ah, bh, start=start, stop=False)
                nc.tensor.matmul(o, ah, bl, start=False, stop=False)
                return nc.tensor.matmul(o, al, bh, start=False, stop=stop)

            for st in steps:
                kind, a = st[0], st[1:]
                if st in ring_use:
                    wait_free(pe, st)
                if kind == "bias":
                    pe.wait_ge(rows_loaded, 64)
                    pe.wait_ge(consts_ready, 1)
                    nc.tensor.transpose(ps(st)[:, 0:49], rows[:, :], ident[0:49, 0:49]).then_inc(full["C"], 1)
                elif kind == "xT":
                    r, b, ring = a
                    pe.wait_ge(tok_ready, tok_writes[("norm", r, b)])
                    pe.wait_ge(consts_ready, 1)
                    for t in range(TB):
                        last = nc.tensor.transpose(ps(st)[:, t * P:(t + 1) * P], tok[:, t, :], ident[:, :])
                    last.then_inc(full[ring], 1)
                elif kind == "gate":
                    r, b = a
                    if r == FFN2 and b == 0:
                        pe.wait_ge(kvd_ready, NB)
                        pe.wait_ge(oT_ready, NB)
                    pe.wait_ge(xT_ready, place[("xT", r, b, "A" if ("xT", r, b, "A") in place else "C")] + 1)
                    pe.wait_ge(gw_ready, 2)
                    for t in range(TB):
                        o = ps(st)[:, t * E:(t + 1) * E]
                        th = xh[:, b, t * P:(t + 1) * P]
                        tl = xl[:, b, t * P:(t + 1) * P]
                        nc.tensor.matmul(o, th, gwh[:, :], start=True, stop=False)
                        nc.tensor.matmul(o, th, gwl[:, :], start=False, stop=False)
                        nc.tensor.matmul(o, tl, gwh[:, :], start=False, stop=False)
                        last = nc.tensor.matmul(o, tl, gwl[:, :], start=False, stop=True)
                    last.then_inc(full["C"], 1)
                elif kind == "probsT":
                    pe.wait_ge(probs_ready, place[st] + 1)
                    nc.tensor.transpose(ps(st)[0:E * TB, 0:P], probs[:, :, :].rearrange("p e t -> p (e t)"),
                                        ident[:, :]).then_inc(full["C"], 1)
                elif kind == "up":
                    r, b, s = a
                    e, c = divmod(s, HC)
                    if s == 0:
                        pe.wait_ge(xT_ready, place[("xT", r, b, "A" if ("xT", r, b, "A") in place else "C")] + 1)
                    if r == FFN1 and b == 0 and c == 0:
                        pe.wait_ge(w_ready, e + 1)
                    wh = Wh[:, e, 0, c * P:(c + 1) * P]
                    wl = Wl[:, e, 0, c * P:(c + 1) * P]
                    for j in range(2):
                        cs = slice(j * BANK, (j + 1) * BANK)
                        last = split3(ps(st)[:, cs], wh, wl, xh[:, b, cs], xl[:, b, cs], True, True)
                    last.then_inc(full["A"], 1)
                elif kind == "down":
                    r, b, s = a
                    e, c = divmod(s, HC)
                    g = expert_no(r, b, e)
                    k = blocks_before(r, b) * E * HC + s
                    pe.wait_ge(hl_ready, k + 1)
                    if r == FFN2 and b == 0 and s == 0:
                        pe.wait_ge(kvd_ready, NB)
                    wh = Wh[:, e, 1, c * P:(c + 1) * P]
                    wl = Wl[:, e, 1, c * P:(c + 1) * P]
                    for j in range(2):
                        cs = slice(j * BANK, (j + 1) * BANK)
                        if c == 0 and g > 0:
                            pe.wait_ge(b_free, 2 * (g - 1) + j + 1)
                        last = split3(psB[:, j, :], wh, wl, hh[:, k % 2, cs], hl[:, k % 2, cs], c == 0, c == HC - 1)
                        if c == HC - 1 and j == 0:
                            last.then_inc(b_full, 1)
                    last.then_inc(down_done, 1)
                elif kind == "accT":
                    r, b, ring = a
                    pe.wait_ge(acc_added, (blocks_before(r, b) + 1) * E)
                    for t in range(TB):
                        last = nc.tensor.transpose(ps(st)[:, t * P:(t + 1) * P], acc[:, b, t * P:(t + 1) * P], ident[:, :])
                    last.then_inc(full[ring], 1)
                elif kind in ("K", "V"):
                    n, i = a
                    if kind == "K" and i == 0 and n % 2 == 0:
                        b = n // 2
                        pe.wait_ge(xT_ready, place[("xT", ATT, b, "A" if b else "C")] + 1)
                        pe.wait_ge(w_ready, WU)
                    ts_ = slice((ST * (n % 2) + i) * P, (ST * (n % 2) + i + 1) * P)
                    u = 1 if kind == "K" else 2
                    for j in range(2):
                        cs = slice(j * BANK, (j + 1) * BANK)
                        last = split3(ps(st)[:, cs], xh[:, n // 2, ts_], xl[:, n // 2, ts_], Ah[:, u, cs], Al[:, u, cs], True, True)
                    last.then_inc(full["A"], 1)
                elif kind == "Q":
                    n, j = a
                    cs = slice((n % 2) * BANK, (n % 2 + 1) * BANK)
                    for q in range(2):
                        c = 2 * j + q
                        last = split3(ps(st)[:, q * BANK:(q + 1) * BANK], Ah[:, 0, c * P:(c + 1) * P], Al[:, 0, c * P:(c + 1) * P],
                                      xh[:, n // 2, cs], xl[:, n // 2, cs], True, True)
                    last.then_inc(full["A"], 1)
                elif kind == "kv":
                    n, i = a
                    ti = ST * n + i
                    pe.wait_ge(feature_ready, feature_use[("K", n, i)] + 1)
                    pe.wait_ge(v_ready, ti + 1)
                    if i == 0 and n == 0:
                        pe.wait_ge(b_free, 2 * 2 * E)
                        wait_left(pe, last_c)
                    if i == 0 and n > 0:
                        pe.wait_ge(kvd_ready, n)
                    for c in range(HP):
                        last = nc.tensor.matmul(kv_ps(c), km[:, ti % 2, c * P:(c + 1) * P], vt[:, ti % 2, c, :],
                                                start=(i == 0 and c % 3 == 0), stop=(i == ST - 1), skip_group_check=True)
                    last.then_inc(kv_done, 1)
                elif kind == "kvT":
                    n, = a
                    pe.wait_ge(kvd_ready, n + 1)
                    for c in range(HP):
                        last = nc.tensor.transpose(ps(st)[:, c * P:(c + 1) * P], kvd[:, c, :], ident[:, :])
                    last.then_inc(full["A"], 1)
                elif kind == "G":
                    n, = a
                    pe.wait_ge(kvT_ready, n + 1)
                    pe.wait_ge(att_loaded, 48)
                    for c in range(HP):
                        last = nc.tensor.matmul(ps(st)[:, c * P:(c + 1) * P], kvTs[:, c, :], wo_sb[:, c, :], start=True, stop=True)
                    last.then_inc(full["A"], 1)
                elif kind == "den":
                    n, = a
                    pe.wait_ge(kvd_ready, n + 1)
                    pe.wait_ge(feature_ready, feature_use[("Q", n, 3)] + 1)
                    if n > 0:
                        pe.wait_ge(oT_ready, n)
                    for c in range(HP):
                        last = nc.tensor.matmul(psC[0:16, 1, :], ksum[:, 16 * c:16 * (c + 1)], qm[:, c, :],
                                                start=(c == 0), stop=(c == HP - 1))
                    last.then_inc(den_full, 1)
                elif kind == "z":
                    n, j = a
                    pe.wait_ge(z_ready, n + 1)
                    for q in range(2):
                        c = 2 * j + q
                        last = nc.tensor.matmul(ps(st)[:, q * BANK:(q + 1) * BANK], pick[:, c, :], z2[:, :], start=True, stop=True)
                    last.then_inc(full["A"], 1)
                elif kind == "out":
                    n, j = a
                    pe.wait_ge(qz_ready, HP // 2 * n + j + 1)
                    pe.wait_ge(G_ready, n + 1)
                    if j == 0:
                        pe.wait_ge(den_read, n + 1)
                    for c in (2 * j, 2 * j + 1):
                        last = nc.tensor.matmul(psC[:, 1, :], Gs[:, c, :], qm[:, c, :], start=(c == 0), stop=(c == HP - 1))
                    if j == 3:
                        last.then_inc(out_done, 1)
                elif kind == "oT":
                    n, = a
                    pe.wait_ge(oT_ready, n + 1)
                    for t in range(ST):
                        last = nc.tensor.transpose(ps(st)[:, t * P:(t + 1) * P], oT[:, t * P:(t + 1) * P], ident[:, :])
                    last.then_inc(full["A"], 1)

        @block.scalar
        def _(act):
            for st in steps:
                kind, a = st[0], st[1:]
                if kind == "W" and a[0] == 0:
                    act.wait_ge(stage_loaded[0], 32)
                    nc.scalar.copy(Wh[:, 0, :, :], stage[:, 0, :, :]).then_inc(hi_split, 1)
                elif kind == "bias":
                    wait_full(act, st)
                    nc.scalar.copy(cols[:, :], ps(st)[:, 0:49]).then_inc(cols_ready, 1)
                elif kind == "xT":
                    r, b, ring = a
                    wait_full(act, st)
                    if r == ATT:
                        act.wait_ge(down_done, (b + 1) * E * HC)
                    if r == FFN2:
                        act.wait_ge(full["A"], ring_use[("Q", 2 * b + 1, 3)][1] + 1)
                    nc.scalar.copy(xh[:, b, :], ps(st)).then_inc(xh_ready, 1)
                elif kind == "probs":
                    act.wait_ge(logits_ready, place[st] + 1)
                    nc.scalar.activation(gX[:, :, :], gB[:, :, :], ACT.Exp, scale=1.0 / TEMP).then_inc(exp_ready, 1)
                elif kind == "up":
                    r, b, s = a
                    k = blocks_before(r, b) * E * HC + s
                    if k == 0:
                        act.wait_ge(cols_ready, 1)
                        act.wait_ge(consts_ready, 1)
                    wait_full(act, st)
                    if k >= 2:
                        act.wait_ge(down_done, k - 1)
                        act.wait_ge(hl_ready, k - 1)
                    bias = cols[:, s:s + 1]
                    nc.scalar.activation(hh[:, k % 2, :], ps(st), ACT.Gelu, bias=bias)
                    nc.scalar.activation(hid[:, k % 2, :], ps(st), ACT.Gelu, bias=bias).then_inc(hid_ready, 1)
                elif kind == "accT":
                    r, b, ring = a
                    wait_full(act, st)
                    earlier = [s2 for s2 in steps[:at[st]] if s2[0] == "xT"]
                    act.wait_ge(full[ring_use[earlier[-1]][0]], ring_use[earlier[-1]][1] + 1)
                    if place[st]:
                        act.wait_ge(x_ready, x_writes[[s2 for s2 in steps[:at[st]] if s2[0] == "addin"][-1]])
                    nc.scalar.copy(tok[:, :, :].rearrange("p t d -> p (t d)"), ps(st)).then_inc(acc_in_tok, 1)
                elif kind == "attention":
                    act.wait_ge(down_done, 2 * E * HC)
                    act.wait_ge(hl_ready, 2 * E * HC)
                    act.wait_ge(acc_added, 2 * E)
                    act.wait_ge(w_ready, WU)
                elif kind == "K":
                    n, i = a
                    k = feature_use[st]
                    act.wait_ge(R_ready, ST * n + i + 1)
                    if k >= 2:
                        act.wait_ge(feature_ready, k - 1)
                    nc.scalar.activation(X[:, k % 2, :], R[:, k % 2, :], ACT.Exp)
                    nc.scalar.activation(R[:, k % 2, :], R[:, k % 2, :], ACT.Relu).then_inc(X_ready, 1)
                elif kind == "Q":
                    n, j = a
                    k = feature_use[st]
                    wait_full(act, st)
                    act.wait_ge(feature_ready, k - 1)
                    for q in range(2):
                        cs = slice(q * BANK, (q + 1) * BANK)
                        bias = cols[:, 40 + 2 * j + q:41 + 2 * j + q]
                        nc.scalar.activation(X[:, k % 2, cs], ps(st)[:, cs], ACT.Exp, bias=bias)
                        last = nc.scalar.activation(R[:, k % 2, cs], ps(st)[:, cs], ACT.Relu, bias=bias)
                    last.then_inc(X_ready, 1)
                elif kind == "kvout":
                    n, = a
                    act.wait_ge(kv_done, ST * (n + 1))
                    act.wait_ge(consts_ready, 1)
                    if n > 0:
                        act.wait_ge(den_full, n)
                    for hf in range(2):
                        ps_ = slice(64 * hf, 64 * hf + 64)
                        B3 = psB[ps_, :, 0:3 * (P + 1)].rearrange("p a (c m) -> p a c m", c=3)
                        C2 = psC[ps_, 0, 0:2 * (P + 1)].rearrange("p (c m) -> p c m", c=2)
                        cs = slice(64 * hf, 64 * hf + 64)
                        nc.scalar.copy(kvd[ps_, 0:6, cs].rearrange("p (a c) m -> p a c m", a=2), B3[:, :, :, cs])
                        nc.scalar.copy(kvd[ps_, 6:8, cs], C2[:, :, cs])
                        nc.scalar.copy(ksum[ps_, hf:hf + 91:18].rearrange("p (a c) -> p a c", a=2), B3[:, :, :, P])
                        last = nc.scalar.copy(ksum[ps_, 108 + hf:108 + hf + 19:18], C2[:, :, P])
                    last.then_inc(kvd_ready, 1)
                elif kind == "kvT":
                    n, = a
                    wait_full(act, st)
                    nc.scalar.copy(kvTs[:, :, :].rearrange("p c m -> p (c m)"), ps(st)).then_inc(kvT_ready, 1)
                elif kind == "G":
                    n, = a
                    wait_full(act, st)
                    if n > 0:
                        act.wait_ge(out_done, n)
                    nc.scalar.copy(Gs[:, :, :].rearrange("p c m -> p (c m)"), ps(st)).then_inc(G_ready, 1)
                elif kind == "outc":
                    n, = a
                    act.wait_ge(out_done, n + 1)
                    if n > 0:
                        act.wait_ge(full["A"], ring_use[("oT", n - 1)][1] + 1)
                    nc.scalar.activation(oT[:, :], psC[:, 1, :], ACT.Identity, bias=cols[:, 48:49]).then_inc(oT_ready, 1)
                elif kind == "ffn2":
                    act.wait_ge(out_done, NB)
                    act.wait_ge(full["A"], ring_use[("oT", NB - 1)][1] + 1)

        @block.vector
        def _(dve):
            link_count = [0]

            def link(ins):
                link_count[0] += 1
                ins.then_inc(dve_chain, 1)
                dve.wait_ge(dve_chain, link_count[0])

            def block_stats(src):
                for t in range(TB):
                    last = nc.vector.bn_stats(bst[:, t, :], src(t))
                link(last)
                for t in range(TB):
                    last = nc.vector.bn_aggr(mv[:, t, :], bst[:, t, :])
                last.then_inc(stats_ready, 1)

            def bc(v):
                return v.unsqueeze(2).to_broadcast([P, TB, E])

            for st in steps:
                kind, a = st[0], st[1:]
                if kind == "W" and a[0] == 0:
                    dve.wait_ge(small_loaded, 32)
                    link(nc.vector.tensor_copy(gwh[:, :], gw[:, :]))
                    nc.vector.tensor_tensor(gwl[:, :], gw[:, :], gwh[:, :].bitcast(F32), ALU.subtract).then_inc(gw_ready, 2)
                elif kind == "stats":
                    r, b = a
                    if r == FFN1:
                        dve.wait_ge(x_loaded[b], 16)
                    else:
                        dve.wait_ge(x_ready, x_writes[x_parts(r, b)])
                    block_stats(lambda t: x[:, b * TB + t, :])
                    if r == FFN1 and b == 0:
                        dve.wait_ge(hi_split, 1)
                        nc.vector.tensor_tensor(Wl[:, 0, :, :], stage[:, 0, :, :], Wh[:, 0, :, :].bitcast(F32),
                                                ALU.subtract).then_inc(w_ready, 1)
                elif kind == "norm":
                    r, b = a
                    dve.wait_ge(rstd_ready, place[("stats", r, b)] + 1 + sum(s2[0] == "accT" for s2 in steps[:at[("stats", r, b)]]))
                    earlier = [s2 for s2 in steps[:at[st]] if s2[0] == "xT"]
                    if earlier:
                        dve.wait_ge(full[ring_use[earlier[-1]][0]], ring_use[earlier[-1]][1] + 1)
                    for t in range(TB):
                        last = nc.vector.tensor_scalar(tok[:, t, :], x[:, b * TB + t, :], mv[:, t, 0:1], rstd[:, t:t + 1],
                                                       ALU.subtract, ALU.mult)
                    last.then_inc(tok_ready, 1)
                elif kind == "xT":
                    r, b, ring = a
                    dve.wait_ge(xh_ready, place[st] + 1)
                    nc.vector.tensor_tensor(xl[:, b, :], ps(st), xh[:, b, :].bitcast(F32), ALU.subtract).then_inc(xT_ready, 1)
                elif kind == "gate":
                    r, b = a
                    wait_full(dve, st)
                    link(nc.vector.tensor_tensor(gL[:, :, :], ps(st)[:, 0:TB * E].rearrange("p (t e) -> p t e", t=TB),
                                                 gb[:, :].unsqueeze(1).to_broadcast([P, TB, E]), ALU.add))
                    rank = order[:, :].unsqueeze(1).to_broadcast([P, TB, E])
                    link(nc.vector.tensor_reduce(gm1[:, :], gL[:, :, :], AX_X, ALU.max))
                    link(nc.vector.tensor_tensor(gA[:, :, :], gL[:, :, :], bc(gm1[:, :]), ALU.is_equal))
                    link(nc.vector.tensor_tensor(gA[:, :, :], gA[:, :, :], rank, ALU.mult))
                    link(nc.vector.tensor_reduce(gm2[:, :], gA[:, :, :], AX_X, ALU.max))
                    link(nc.vector.tensor_tensor(gS[:, :, :], gA[:, :, :], bc(gm2[:, :]), ALU.is_equal))
                    link(nc.vector.scalar_tensor_tensor(gA[:, :, :], gS[:, :, :], FAR, gL[:, :, :], ALU.mult, ALU.add))
                    link(nc.vector.tensor_reduce(gm2[:, :], gA[:, :, :], AX_X, ALU.max))
                    link(nc.vector.tensor_tensor(gA[:, :, :], gA[:, :, :], bc(gm2[:, :]), ALU.is_equal))
                    link(nc.vector.tensor_tensor(gA[:, :, :], gA[:, :, :], rank, ALU.mult))
                    link(nc.vector.tensor_reduce(gm2[:, :], gA[:, :, :], AX_X, ALU.max))
                    link(nc.vector.tensor_tensor(gA[:, :, :], gA[:, :, :], bc(gm2[:, :]), ALU.is_equal))
                    link(nc.vector.tensor_tensor(gS[:, :, :], gS[:, :, :], gA[:, :, :], ALU.add))
                    nc.vector.tensor_tensor(gB[:, :, :], gL[:, :, :], bc(gm1[:, :]), ALU.subtract).then_inc(logits_ready, 1)
                elif kind == "probs":
                    dve.wait_ge(exp_ready, place[st] + 1)
                    link(nc.vector.tensor_tensor(gA[:, :, :], gX[:, :, :], gS[:, :, :], ALU.mult))
                    link(nc.vector.tensor_reduce(gsum[:, :], gA[:, :, :], AX_X, ALU.add))
                    link(nc.vector.reciprocal(gsum[:, :], gsum[:, :]))
                    nc.vector.tensor_tensor(probs[:, :, :].rearrange("p e t -> p t e"), gA[:, :, :], bc(gsum[:, :]),
                                            ALU.mult).then_inc(probs_ready, 1)
                elif kind == "probsT":
                    wait_full(dve, st)
                    if place[st]:
                        dve.wait_ge(table_stored, 16 * place[st])
                    nc.vector.tensor_copy(pT[:, :], ps(st)[0:E * TB, 0:P]).then_inc(pT_ready, 1)
                elif kind == "up":
                    r, b, s = a
                    k = blocks_before(r, b) * E * HC + s
                    dve.wait_ge(hid_ready, k + 1)
                    if k >= 2:
                        dve.wait_ge(down_done, k - 1)
                    nc.vector.tensor_tensor(hl[:, k % 2, :], hid[:, k % 2, :], hh[:, k % 2, :].bitcast(F32),
                                            ALU.subtract).then_inc(hl_ready, 1)
                elif kind == "down" and a[2] % HC == HC - 1:
                    r, b, s = a
                    e = s // HC
                    g = expert_no(r, b, e)
                    k = blocks_before(r, b) * E * HC + s
                    dve.wait_ge(pb_loaded[g % 2], 16 * (g // 2 + 1))
                    if e == 0 and (r, b) != (FFN1, 0) and (r, b) != (FFN1, 1):
                        pr = ("accT", FFN1, b, "A" if b else "C")
                        dve.wait_ge(full[pr[3]], ring_use[pr][1] + 1)
                    if g >= 2:
                        dve.wait_ge(acc_added, g - 1)
                    for j in range(2):
                        cs = slice(j * BANK, (j + 1) * BANK)
                        if j == 0:
                            dve.wait_ge(b_full, g + 1)
                        else:
                            dve.wait_ge(down_done, k + 1)
                        dst = acc[:, b, cs] if e == 0 else gated[:, g % 2, cs]
                        last = nc.vector.scalar_tensor_tensor(dst, psB[:, j, :], cols[:, 32 + e:33 + e], pb[:, g % 2, cs],
                                                              ALU.add, ALU.mult)
                        last.then_inc(b_free, 1)
                elif kind == "accT":
                    r, b, ring = a
                    dve.wait_ge(acc_in_tok, place[st] + 1)
                    block_stats(lambda t: tok[:, t, :])
                elif kind == "addin":
                    r, b = a
                    me = [s2 for s2 in steps if s2[0] == "accT" and s2[1:3] == (r, b)][0]
                    dve.wait_ge(rstd_ready, 1 + sum(s2[0] in ("accT", "stats") for s2 in steps[:at[me]]))
                    for t in range(TB):
                        last = nc.vector.tensor_scalar(tok[:, t, :], tok[:, t, :], mv[:, t, 0:1], rstd[:, t:t + 1],
                                                       ALU.subtract, ALU.mult)
                    link(last)
                    link(nc.vector.tensor_tensor(tok[:, :, :], tok[:, :, :], gain[:, :].unsqueeze(1).to_broadcast([P, TB, P]),
                                                 ALU.mult))
                    xb = x[:, b * TB:(b + 1) * TB, :]
                    dve.wait_ge(x_shifted, blocks_before(r, b) + 1)
                    nc.vector.tensor_tensor(xb, xb, tok[:, :, :], ALU.add).then_inc(x_ready, 1)
                elif kind == "attention":
                    dve.wait_ge(down_done, 2 * E * HC)
                    dve.wait_ge(acc_added, 2 * E)
                    dve.wait_ge(w_ready, WU)
                    dve.wait_ge(att_loaded, 48)
                    link(nc.vector.memset(z2[:, :].bitcast(F32), 0.0))
                elif kind == "K":
                    n, i = a
                    k = feature_use[st]
                    wait_full(dve, st)
                    nc.vector.tensor_tensor(R[:, k % 2, :], ps(st), bkv[:, 0, :], ALU.add).then_inc(R_ready, 1)
                elif kind == "V":
                    n, i = a
                    ti = ST * n + i
                    wait_full(dve, st)
                    if ti >= 2:
                        dve.wait_ge(kv_done, ti - 1)
                    nc.vector.tensor_tensor(vt[:, ti % 2, :, 0:P], ps(st).rearrange("p (c m) -> p c m", c=HP),
                                            bkv[:, 1, :].rearrange("p (c m) -> p c m", c=HP), ALU.add).then_inc(v_ready, 1)
                elif kind in ("Kf", "Qf"):
                    n, i = a
                    k = feature_use[(kind[0], n, i)]
                    dve.wait_ge(X_ready, k + 1)
                    if kind == "Kf":
                        ti = ST * n + i
                        if ti >= 2:
                            dve.wait_ge(kv_done, ti - 1)
                        dst = km[:, ti % 2, :]
                    else:
                        if n > 0:
                            dve.wait_ge(out_done, n)
                        dst = qm[:, 2 * i:2 * i + 2, :].rearrange("p c n -> p (c n)")
                    nc.vector.scalar_tensor_tensor(dst, X[:, k % 2, :], 1.0, R[:, k % 2, :], ALU.min, ALU.add)\
                        .then_inc(feature_ready, 1)
                elif kind == "denz":
                    n, = a
                    dve.wait_ge(den_full, n + 1)
                    if n > 0:
                        dve.wait_ge(full["A"], ring_use[("oT", n - 1)][1] + 1)
                    nc.vector.tensor_scalar(zr[:, :], psC[0:16, 1, :], ATT_EPS, None, ALU.add).then_inc(den_read, 1)
                    dve.wait_ge(den_read, n + 1)
                    link(nc.vector.reciprocal(zr[:, :], zr[:, :]))
                    if n > 0:
                        dve.wait_ge(full["A"], ring_use[("z", n - 1, 3)][1] + 1)
                    link(nc.vector.tensor_copy(z2[0:16, :], zr[:, :]))
                    nc.vector.tensor_tensor(z2[32:48, :], zr[:, :], z2[0:16, :].bitcast(F32), ALU.subtract).then_inc(z_ready, 1)
                elif kind == "z":
                    n, j = a
                    wait_full(dve, st)
                    q2 = qm[:, 2 * j:2 * j + 2, :].rearrange("p c n -> p (c n)")
                    nc.vector.tensor_tensor(q2, q2, ps(st), ALU.mult).then_inc(qz_ready, 1)
                elif kind == "oT":
                    n, = a
                    wait_full(dve, st)
                    xb = x[:, ST * n:ST * (n + 1), :]
                    nc.vector.tensor_tensor(xb, xb, ps(st)[:, 0:BANK].rearrange("p (t d) -> p t d", t=ST),
                                            ALU.add).then_inc(x_ready, 1)
                elif kind == "ffn2":
                    dve.wait_ge(out_done, NB)

        @block.gpsimd
        def _(pool):
            link_count = [0]

            def link(ins):
                link_count[0] += 1
                ins.then_inc(pool_chain, 1)
                pool.wait_ge(pool_chain, link_count[0])

            link(nc.gpsimd.memset(ident[:, :], 0.0))
            link(nc.gpsimd.affine_select(out=ident[:, :], in_=ident[:, :], compare_op=ALU.not_equal, fill=1.0, base=0,
                                         pattern=[[-1, P]], channel_multiplier=1))
            nc.gpsimd.memset(half[:, :], -0.5)
            link(nc.gpsimd.memset(hid[0:48, 0, :], 0.0))
            for row in (0, 32):
                v = hid[0:48, 0, :].rearrange("k (c j m) -> k c j m", c=HP, j=2)
                link(nc.gpsimd.affine_select(out=v, in_=v, compare_op=ALU.not_equal, fill=1.0, base=-row,
                                             pattern=[[-2, HP], [-1, 2], [0, P // 2]], channel_multiplier=1))
            nc.gpsimd.tensor_copy(pick[:, :, :].rearrange("k c m -> k (c m)"), hid[0:48, 0, :])
            for e in range(E):
                nc.gpsimd.memset(order[:, e:e + 1], float(E - e))
            nc.gpsimd.memset(vt[:, :, :, P:P + 1], 1.0)
            nc.gpsimd.memset(ksum[:, :], 0.0)
            nc.gpsimd.memset(kvd[:, :, :], 0.0).then_inc(consts_ready, 1)
            for st in steps:
                kind, a = st[0], st[1:]
                if kind in ("stats", "accT"):
                    n = sum(s2[0] in ("accT", "stats") for s2 in steps[:at[st]])
                    pool.wait_ge(stats_ready, n + 1)
                    link(nc.gpsimd.tensor_scalar(ve[:, :], mv[:, :, 1], LN_EPS, 1.0, ALU.add, ALU.mult))
                    nc.gpsimd.tensor_tensor(rstd[:, :], ve[:, :], half[:, :], ALU.pow).then_inc(rstd_ready, 1)
                    if kind == "stats" and st[1:] == (FFN1, 0):
                        pool.wait_ge(ln_loaded, 32)
                        link(nc.gpsimd.tensor_scalar(gain[:, :], gain[:, :], 0.5, 1.0, ALU.mult, ALU.mult))
                        link(nc.gpsimd.tensor_scalar(shift[:, :], shift[:, :], 0.5, 1.0, ALU.mult, ALU.mult))
                if kind == "W" and a[0] > 0:
                    u, = a
                    pool.wait_ge(stage_loaded[u % 2], 32 * (u // 2 + 1))
                    s = stage[:, u % 2, :, :]
                    h, l = (Wh[:, u, :, :], Wl[:, u, :, :]) if u < E else (
                        Ah[:, u - E, :].rearrange("p (a n) -> p a n", a=2), Al[:, u - E, :].rearrange("p (a n) -> p a n", a=2))
                    link(nc.gpsimd.tensor_copy(h, s))
                    if u == 1:
                        pool.wait_ge(w_ready, 1)
                    nc.gpsimd.tensor_tensor(l, s, h.bitcast(F32), ALU.subtract).then_inc(w_ready, 1)
                elif kind == "norm" and a[0] != ATT:
                    r, b = a
                    pool.wait_ge(tok_ready, tok_writes[st])
                    xb = x[:, b * TB:(b + 1) * TB, :]
                    nc.gpsimd.tensor_tensor(xb, xb, shift[:, :].unsqueeze(1).to_broadcast([P, TB, P]), ALU.add)\
                        .then_inc(x_shifted, 1)
                elif kind == "down" and a[2] % HC == HC - 1:
                    r, b, s = a
                    e = s // HC
                    g = expert_no(r, b, e)
                    pool.wait_ge(b_free, 2 * (g + 1))
                    if g:
                        pool.wait_ge(acc_added, g)
                    if e == 0:
                        pool.engine_nop().then_inc(acc_added, 1)
                    else:
                        nc.gpsimd.tensor_tensor(acc[:, b, :], acc[:, b, :], gated[:, g % 2, :], ALU.add).then_inc(acc_added, 1)


_INS = ['L0_attn_x', 'L0_attn_wq', 'L0_attn_bq', 'L0_attn_wk', 'L0_attn_bk', 'L0_attn_wv', 'L0_attn_bv', 'L0_attn_wo',
        'L0_attn_bo', 'L0_ffn_gate_w', 'L0_ffn_gate_b', 'L0_ffn_w1', 'L0_ffn_b1', 'L0_ffn_w2', 'L0_ffn_b2',
        'L0_ffn_ln_g', 'L0_ffn_ln_b']
_OUTS = [((4, 512, 128), 'float32')]


def kernel(**inputs):
    import numpy as _np
    import concourse.bacc as _bacc
    from concourse import mybir as _mybir
    from concourse.bass_utils import run_bass_kernel_spmd as _run

    nc = _bacc.Bacc("TRN2", target_bir_lowering=False, num_devices=1)
    arrays, args = {}, []
    for name in _INS:
        a = _np.ascontiguousarray(inputs[name])
        arrays[f"in_{name}_dram"] = a
        args.append(nc.dram_tensor(f"in_{name}_dram", a.shape, _mybir.dt.from_np(a.dtype), kind="ExternalInput").ap())
    for i, (shape, dtype) in enumerate(_OUTS):
        dt = _mybir.dt.from_np(_np.dtype(dtype))
        args.append(nc.dram_tensor(f"out_{i}_dram", shape, dt, kind="ExternalOutput").ap())
    bass_macaron_kernel(nc, *args)
    r = _run(nc, [arrays], core_ids=[0])
    got = tuple(r.results[0][f"out_{i}_dram"] for i in range(len(_OUTS)))
    return got[0]
```

```python
from contextlib import ExitStack

import concourse.bass as bass
from concourse import mybir

ALU = mybir.AluOpType
ACT = mybir.ActivationFunctionType
F32 = mybir.dt.float32
F32R = mybir.dt.float32r
AX_X = mybir.AxisListType.X

P = 128
TILES = 16
TB = 8
BLK = TB * P
BANK = 512
E = 8
HC = 4
HP = 8
NB = 4
ST = 4
WU = 11
TEMP = 0.9
LN_EPS = 1e-5
ATT_EPS = 1e-6
FAR = -3.0e38
LAG = 2
HS = LAG + 1
FFN1, ATT, FFN2 = 0, 1, 2


def timeline():
    t = []
    unfinished = []

    def feature(*st):
        t.append(st)
        if st[0] == "K":
            t.append(("V", *st[1:]))
        finish()
        unfinished.append(("Kf" if st[0] == "K" else "Qf", *st[1:]))

    def finish():
        while unfinished:
            t.append(unfinished.pop())

    def rank(r, b, first, last):
        t.extend(("rank", r, b, i) for i in range(first, last))

    def ffn(r, between, first=0):
        for k in range(first, 2 * E * HC):
            b, s = divmod(k, E * HC)
            t.append(("up", r, b, s))
            t.extend(between.get((b, s), ()))
            if k >= LAG:
                t.append(("down", r, *divmod(k - LAG, E * HC)))
            t.append(("low", r, b, s))

    t += [("W", 0), ("stats", FFN1, 0), ("norm", FFN1, 0), ("xT", FFN1, 0, "C"), ("W0",), ("W", 1), ("bias",),
          ("gate", FFN1, 0, "C")]
    rank(FFN1, 0, 0, 2)
    between = {(0, HC * e): [("W", e + 2)] for e in range(E)}
    between[0, 0] += [("rank", FFN1, 0, 2), ("rank", FFN1, 0, 3), ("probs", FFN1, 0)]
    between[0, 1] = [("probsT", FFN1, 0, "C")]
    between[0, 30] = [("W", 10)]
    between[0, 6] = [("stats", FFN1, 1)]
    between[0, 7] = [("norm", FFN1, 1)]
    between[0, 9] = [("xT", FFN1, 1, "C")]
    between[0, 11] = [("gate", FFN1, 1, "C")]
    for i in range(4):
        between.setdefault((0, 12 + i), []).append(("rank", FFN1, 1, i))
    between[0, 17] = [("probs", FFN1, 1)]
    between[0, 19] = [("probsT", FFN1, 1, "C")]
    between[1, 2] = [("kvbias",)]
    between[1, 4] = [("accT", FFN1, 0, "C")]
    between[1, 7] = [("addin", FFN1, 0)]
    between[1, 10] = [("stats", ATT, 0)]
    between[1, 12] = [("norm", ATT, 0)]
    between[1, 14] = [("xT", ATT, 0, "C")]
    ffn(FFN1, between)

    b_last = E * HC - 1
    t += [("K", 0, 0), ("down", FFN1, 1, b_last - 1), ("V", 0, 0), ("down", FFN1, 1, b_last)]
    unfinished.append(("Kf", 0, 0))
    feature("K", 0, 1)
    feature("Q", 0, 0)
    t += [("kv", 0, 0), ("accT", FFN1, 1, "A")]
    feature("K", 0, 2)
    feature("Q", 0, 1)
    t += [("kv", 0, 1)]
    feature("K", 0, 3)
    t += [("addin", FFN1, 1)]
    feature("Q", 0, 2)
    t += [("kv", 0, 2)]
    feature("Q", 0, 3)
    t += [("kv", 0, 3), ("kvout", 0)]
    for n in range(NB - 1):
        m = n + 1
        finish()
        feature("K", m, 0)
        t += [("kvT", n)]
        finish()
        t += [("den", n, 0), ("denz", n, 0), ("den", n, 1), ("kv", m, 0), ("denz", n, 1)]
        feature("K", m, 1)
        t += [("G", n), ("z", n, 0)]
        feature("K", m, 2)
        t += [("out", n, 0), ("z", n, 1), ("kv", m, 1)]
        feature("Q", m, 0)
        t += [("out", n, 1), ("z", n, 2)]
        feature("Q", m, 1)
        t += [("out", n, 2), ("z", n, 3)]
        feature("Q", m, 2)
        if n == 0:
            t += [("stats", ATT, 1)]
        feature("K", m, 3)
        t += [("out", n, 3), ("outc", n), ("kv", m, 2)]
        if n == 0:
            t += [("norm", ATT, 1)]
        feature("Q", m, 3)
        if n == 0:
            t += [("xT", ATT, 1, "A")]
        if n == 2:
            t += [("xT", FFN2, 0, "A")]
        t += [("oT", n), ("kv", m, 3), ("kvout", m)]
        if n == 1:
            t += [("stats", FFN2, 0), ("norm", FFN2, 0)]
    n = NB - 1
    finish()
    t += [("gate", FFN2, 0, "A"), ("den", n, 0)]
    rank(FFN2, 0, 0, 2)
    t += [("denz", n, 0), ("den", n, 1)]
    rank(FFN2, 0, 2, 4)
    t += [("probs", FFN2, 0), ("denz", n, 1), ("kvT", n), ("G", n), ("probsT", FFN2, 0, "A"), ("up", FFN2, 0, 0),
          ("z", n, 0), ("z", n, 1), ("low", FFN2, 0, 0), ("out", n, 0), ("z", n, 2), ("out", n, 1), ("z", n, 3),
          ("up", FFN2, 0, 1), ("out", n, 2), ("out", n, 3), ("low", FFN2, 0, 1), ("outc", n)]

    between = {(0, 2): [("oT", n)], (0, 4): [("stats", FFN2, 1)], (0, 6): [("norm", FFN2, 1)], (0, 8): [("xT", FFN2, 1, "C")],
               (0, 10): [("gate", FFN2, 1, "C")], (0, 16): [("probs", FFN2, 1)], (0, 18): [("probsT", FFN2, 1, "C")],
               (1, 4): [("accT", FFN2, 0, "C")], (1, 7): [("addin", FFN2, 0)]}
    for i in range(4):
        between[0, 12 + i] = [("rank", FFN2, 1, i)]
    ffn(FFN2, between, LAG)
    t += [("down", FFN2, 1, b_last - 1), ("down", FFN2, 1, b_last), ("accT", FFN2, 1, "C"), ("addin", FFN2, 1)]
    return t


def bass_macaron_kernel(nc: bass.Bass, x_in, wq, bq, wk, bk, wv, bv, wo, bo, gate_w, gate_b,
                        w1, b1, w2, b2, ln_g, ln_b, out):
    steps = timeline()

    place, ring_use, uses, kinds = {}, {}, {"A": 0, "C": 0}, {}
    feature_use = {}
    for st in steps:
        k = st[0]
        place[st] = kinds.get(k, 0)
        kinds[k] = place[st] + 1
        ring = st[-1] if st[-1] in ("A", "C") else (
            "A" if k in ("up", "K", "V", "Q", "kvT", "G", "z", "oT") else "C" if k == "bias" else None)
        if ring:
            ring_use[st] = (ring, uses[ring])
            uses[ring] += 1
        if k in ("K", "Q"):
            feature_use[st] = len(feature_use)
    assert set(place) == set(steps) and len(place) == len(steps)
    at = {st: i for i, st in enumerate(steps)}
    c_uses_before_attention = sum(1 for st, (r, _) in ring_use.items() if r == "C" and at[st] < at[("K", 0, 0)])

    ctx = ExitStack()
    with ctx:
        def sb(name, shape, dt=F32, scope=ctx):
            return scope.enter_context(nc.sbuf_tensor(name, shape, dt))

        def sem(name):
            return ctx.enter_context(nc.semaphore(name))

        x = sb("x", [P, TILES, P])
        xh = sb("xh", [P, 2, BLK], F32R)
        xl = sb("xl", [P, 2, BLK], F32R)
        Wh = sb("Wh", [P, E, 2, BANK], F32R)
        Wl = sb("Wl", [P, E, 2, BANK], F32R)
        Ah = sb("Ah", [P, 3, 2 * BANK], F32R)
        Al = sb("Al", [P, 3, 2 * BANK], F32R)
        wo_sb = sb("wo_sb", [P, HP, P])
        bkv = sb("bkv", [P, 2, 2 * BANK])
        stage = bkv[:, :, :].rearrange("p s (a n) -> p s a n", a=2)
        acc = sb("acc", [P, 2, BLK])
        vt = sb("vt", [P, 2, HP, P + 1])
        kvd = sb("kvd", [P, HP, P])
        ksum = sb("ksum", [P, HP * 16])
        tok = sb("tok", [P, TB, P])
        ident = sb("ident", [P, P])
        pick = sb("pick", [48, HP, P], F32R)
        gain = sb("gain", [P, P])
        shift = sb("shift", [P, P])
        rows = sb("rows", [49, P])
        cols = sb("cols", [P, 49])
        gw = sb("gw", [P, E])
        gwh = sb("gwh", [P, E], F32R)
        gwl = sb("gwl", [P, E], F32R)
        gb = sb("gb", [P, E])
        order = sb("order", [P, E])
        half = sb("half", [P, TB])
        bst = sb("bst", [P, TB, 6])
        mv = sb("mv", [P, TB, 2])
        ve = sb("ve", [P, TB])
        rstd = sb("rstd", [P, TB])
        gL = sb("gL", [P, TB, E])
        gA = sb("gA", [P, TB, E])
        gB = sb("gB", [P, TB, E])
        gS = sb("gS", [P, TB, E])
        gX = sb("gX", [P, TB, E])
        gm1 = sb("gm1", [P, TB])
        gm2 = sb("gm2", [P, TB])
        gsum = sb("gsum", [P, TB])
        probs = sb("probs", [P, E, TB])
        pT = sb("pT", [E * TB, P])

        ffn_only = ExitStack()
        pb = sb("pb", [P, 2, BLK], scope=ffn_only)
        hh = sb("hh", [P, HS, BLK], F32R, scope=ffn_only)
        hid = sb("hid", [P, 2, BLK], scope=ffn_only)
        hl = sb("hl", [P, HS, BLK], F32R, scope=ffn_only)
        gated = sb("gated", [P, 2, BLK], scope=ffn_only)
        ffn_only.close()
        kvTs = sb("kvTs", [P, HP, P])
        Gs = sb("Gs", [P, HP, P])
        R = sb("R", [P, 2, 2 * BANK])
        X = sb("X", [P, 2, 2 * BANK])
        km = sb("km", [P, 2, 2 * BANK])
        qm = sb("qm", [P, HP, BANK])
        z2 = sb("z2", [48, BANK], F32R)
        oT = acc[:, 0, 0:BANK]
        zr = oT[0:16, :]

        psA = ctx.enter_context(nc.psum_tensor("psA", [P, 2, 2 * BANK], F32))
        psB = ctx.enter_context(nc.psum_tensor("psB", [P, 2, BANK], F32))
        psC = ctx.enter_context(nc.psum_tensor("psC", [P, 2, BANK], F32))

        table = nc.dram_tensor("gate_table", [4, E * TB, P], F32, kind="Internal").ap()

        def ps(st):
            ring, n = ring_use[st]
            return psA[:, n % 2, :] if ring == "A" else psC[:, :, :].rearrange("p a n -> p (a n)")

        def kv_ps(c):
            t = psB[:, c // 3, :] if c < 6 else psC[:, 0, :]
            return t[:, (c % 3) * (P + 1):(c % 3 + 1) * (P + 1)]

        def den_ps(hf):
            return psC[0:16, hf, 0:BANK // 2]

        x_loaded = [sem("x_loaded0"), sem("x_loaded1")]
        small_loaded = sem("small_loaded")
        ln_loaded = sem("ln_loaded")
        rows_loaded = sem("rows_loaded")
        att_loaded = sem("att_loaded")
        stage_loaded = [sem("stage_loaded0"), sem("stage_loaded1")]
        table_stored = sem("table_stored")
        pb_loaded = [sem("pb_loaded0"), sem("pb_loaded1")]
        stored = sem("stored")
        consts_ready = sem("consts_ready")
        hi_split = sem("hi_split")
        w_ready = sem("w_ready")
        gw_ready = sem("gw_ready")
        cols_ready = sem("cols_ready")
        full = {"A": sem("fullA"), "C": sem("fullC")}
        b_full = sem("b_full")
        b_free = sem("b_free")
        stats_ready = sem("stats_ready")
        rstd_ready = sem("rstd_ready")
        tok_ready = sem("tok_ready")
        x_shifted = sem("x_shifted")
        xh_ready = sem("xh_ready")
        xT_ready = sem("xT_ready")
        logits_read = sem("logits_read")
        logits_ready = sem("logits_ready")
        exp_ready = sem("exp_ready")
        probs_ready = sem("probs_ready")
        pT_ready = sem("pT_ready")
        hid_ready = sem("hid_ready")
        hl_ready = sem("hl_ready")
        down_done = sem("down_done")
        gated_ready = sem("gated_ready")
        acc_added = sem("acc_added")
        acc_in_tok = sem("acc_in_tok")
        x_ready = sem("x_ready")
        R_ready = sem("R_ready")
        X_ready = sem("X_ready")
        feature_ready = sem("feature_ready")
        v_ready = sem("v_ready")
        kv_done = sem("kv_done")
        kvd_ready = sem("kvd_ready")
        kvT_ready = sem("kvT_ready")
        G_ready = sem("G_ready")
        den_full = sem("den_full")
        den_read = sem("den_read")
        z_ready = sem("z_ready")
        qz_ready = sem("qz_ready")
        out_done = sem("out_done")
        oT_ready = sem("oT_ready")
        dve_chain = sem("dve_chain")
        pool_chain = sem("pool_chain")

        def wait_full(eng, st):
            ring, n = ring_use[st]
            eng.wait_ge(full[ring], n + 1)

        def wait_left(eng, st):
            kind, a = st[0], st[1:]
            done, n = {
                "bias": (cols_ready, 1),
                "xT": (xT_ready, place[st] + 1),
                "gate": (logits_read, place[st] + 1),
                "probsT": (pT_ready, place[st] + 1),
                "up": (hid_ready, place[st] + 1),
                "accT": (acc_in_tok, place[st] + 1),
                "K": (R_ready, place[st] + 1),
                "V": (v_ready, place[st] + 1),
                "Q": (X_ready, feature_use.get(st, 0) + 1),
                "kvT": (kvT_ready, place[st] + 1),
                "G": (G_ready, place[st] + 1),
                "z": (qz_ready, place[st] + 1),
                "oT": (x_ready, x_writes.get(st, 0)),
            }[kind]
            eng.wait_ge(done, n)

        def wait_free(eng, st):
            ring, n = ring_use[st]
            slots = 2 if ring == "A" else 1
            if n >= slots:
                wait_left(eng, used_by[ring, n - slots])

        def expert_no(r, b, e):
            return (2 * (r == FFN2) + b) * E + e

        def blocks_before(r, b):
            return 2 * (r == FFN2) + b

        def slot(k):
            return (k - 2 * E * HC) % HS

        def x_parts(r, b):
            return {FFN1: None, ATT: ("addin", FFN1, b), FFN2: ("oT", 2 * b + 1)}[r]

        def xT_place(r, b):
            return place[next(st for st in place if st[:3] == ("xT", r, b))]

        def last_use(*kinds_blocks):
            return max(n for st, (ring, n) in ring_use.items() if ring == "A" and any(st[:len(k)] == k for k in kinds_blocks)) + 1

        x_writes = {}
        for st in steps:
            if st[0] in ("addin", "oT"):
                x_writes[st] = len(x_writes) + 1
        tok_writes = {}
        for st in steps:
            if st[0] == "norm":
                tok_writes[st] = sum(k[0] == "norm" for k in tok_writes) + 1

        used_by = {v: st for st, v in ring_use.items()}
        last_c = used_by["C", c_uses_before_attention - 1]

        block = ctx.enter_context(nc.Block())

        @block.sync
        def _(sp):
            x_v = x_in.rearrange("n (t p) d -> p (n t) d", p=P)
            out_v = out.rearrange("n (t p) d -> p (n t) d", p=P)
            w2_v = w2.rearrange("e (c k) d -> e k c d", k=P)
            att_w = [w.rearrange("d h m -> d (h m)") for w in (wq, wk, wv)]
            sp.dma_start(x[:, 0:TB, :], x_v[:, 0:TB, :]).then_inc(x_loaded[0], 16)
            sp.dma_start(gw[:, :], gate_w).then_inc(small_loaded, 16)
            sp.dma_start(gb[:, :], gate_b.partition_broadcast(P)).then_inc(small_loaded, 16)
            sp.dma_start(rows[0:32, :], b1.rearrange("e (c k) -> (e c) k", k=P)).then_inc(rows_loaded, 16)
            sp.dma_start(rows[32:40, :], b2).then_inc(rows_loaded, 16)
            sp.dma_start(rows[40:48, :], bq.rearrange("(c j) m -> c (j m)", j=2)).then_inc(rows_loaded, 16)
            sp.dma_start(rows[48:49, :], bo.rearrange("(a d) -> a d", a=1)).then_inc(rows_loaded, 16)
            for st in steps:
                kind, a = st[0], st[1:]
                if kind == "W":
                    u, = a
                    if u >= 2:
                        sp.wait_ge(w_ready, u - 1)
                    s = stage[:, u % 2, :, :]
                    if u < E:
                        sp.dma_start(s[:, 0, :], w1[u]).then_inc(stage_loaded[u % 2], 16)
                        sp.dma_start(s[:, 1, :].rearrange("k (c d) -> k c d", c=HC), w2_v[u]).then_inc(stage_loaded[u % 2], 16)
                    else:
                        sp.dma_start(s.rearrange("p a n -> p (a n)"), att_w[u - E]).then_inc(stage_loaded[u % 2], 32)
                    if u == 1:
                        sp.dma_start(x[:, TB:TILES, :], x_v[:, TB:TILES, :]).then_inc(x_loaded[1], 16)
                        sp.dma_start(gain[:, :], ln_g.partition_broadcast(P)).then_inc(ln_loaded, 16)
                        sp.dma_start(shift[:, :], ln_b.partition_broadcast(P)).then_inc(ln_loaded, 16)
                    if u == 8:
                        sp.dma_start(wo_sb[:, :, :], wo.rearrange("(c j) m d -> (j m) c d", j=2)).then_inc(att_loaded, 16)
                elif kind == "kvbias":
                    sp.wait_ge(w_ready, WU)
                    sp.dma_start(bkv[:, 0, :], bk.rearrange("h m -> (h m)").partition_broadcast(P)).then_inc(att_loaded, 16)
                    sp.dma_start(bkv[:, 1, :], bv.rearrange("h m -> (h m)").partition_broadcast(P)).then_inc(att_loaded, 16)
                elif kind == "probsT":
                    n = place[st]
                    sp.wait_ge(pT_ready, n + 1)
                    sp.dma_start(table[n], pT[:, :]).then_inc(table_stored, 16)
                elif kind == "down" and a[2] % HC == 0:
                    r, b, s = a
                    e = s // HC
                    g = expert_no(r, b, e)
                    sp.wait_ge(table_stored, 16 * (blocks_before(r, b) + 1))
                    if (r, b, e) == (FFN2, 0, 0):
                        sp.wait_ge(out_done, NB * HP // 2)
                    if g >= 2:
                        sp.wait_ge(b_free, 2 * (g - 1))
                    row = table[blocks_before(r, b), e * TB:(e + 1) * TB, :].rearrange("t p -> (t p)")
                    sp.dma_start(pb[:, g % 2, :], row.partition_broadcast(P)).then_inc(pb_loaded[g % 2], 16)
                elif kind == "addin" and a[0] == FFN2:
                    b = a[1]
                    sp.wait_ge(x_ready, x_writes[st])
                    sp.dma_start(out_v[:, b * TB:(b + 1) * TB, :], x[:, b * TB:(b + 1) * TB, :]).then_inc(stored, 16)
            sp.wait_ge(stored, 32)

        @block.tensor
        def _(pe):
            def split3(o, ah, al, bh, bl, start, stop):
                nc.tensor.matmul(o, ah, bh, start=start, stop=False)
                nc.tensor.matmul(o, ah, bl, start=False, stop=False)
                return nc.tensor.matmul(o, al, bh, start=False, stop=stop)

            for st in steps:
                kind, a = st[0], st[1:]
                if st in ring_use:
                    wait_free(pe, st)
                if kind == "bias":
                    pe.wait_ge(rows_loaded, 64)
                    pe.wait_ge(consts_ready, 1)
                    nc.tensor.transpose(ps(st)[:, 0:49], rows[:, :], ident[0:49, 0:49]).then_inc(full["C"], 1)
                elif kind == "xT":
                    r, b, ring = a
                    pe.wait_ge(tok_ready, tok_writes[("norm", r, b)])
                    pe.wait_ge(consts_ready, 1)
                    if r == FFN2 and b == 1:
                        pe.wait_ge(kvd_ready, NB)
                        pe.wait_ge(oT_ready, NB)
                    for t in range(TB):
                        last = nc.tensor.transpose(ps(st)[:, t * P:(t + 1) * P], tok[:, t, :], ident[:, :])
                    last.then_inc(full[ring], 1)
                elif kind == "gate":
                    r, b, ring = a
                    pe.wait_ge(xT_ready, xT_place(r, b) + 1)
                    pe.wait_ge(gw_ready, 2)
                    for t in range(TB):
                        o = ps(st)[:, t * E:(t + 1) * E]
                        th = xh[:, b, t * P:(t + 1) * P]
                        tl = xl[:, b, t * P:(t + 1) * P]
                        nc.tensor.matmul(o, th, gwh[:, :], start=True, stop=False)
                        nc.tensor.matmul(o, th, gwl[:, :], start=False, stop=False)
                        nc.tensor.matmul(o, tl, gwh[:, :], start=False, stop=False)
                        last = nc.tensor.matmul(o, tl, gwl[:, :], start=False, stop=True)
                    last.then_inc(full[ring], 1)
                elif kind == "probsT":
                    pe.wait_ge(probs_ready, place[st] + 1)
                    nc.tensor.transpose(ps(st)[0:E * TB, 0:P], probs[:, :, :].rearrange("p e t -> p (e t)"),
                                        ident[:, :]).then_inc(full[a[2]], 1)
                elif kind == "up":
                    r, b, s = a
                    e, c = divmod(s, HC)
                    if s == 0:
                        pe.wait_ge(xT_ready, xT_place(r, b) + 1)
                    if r == FFN1 and b == 0 and c == 0:
                        pe.wait_ge(w_ready, e + 1)
                    wh = Wh[:, e, 0, c * P:(c + 1) * P]
                    wl = Wl[:, e, 0, c * P:(c + 1) * P]
                    for j in range(2):
                        cs = slice(j * BANK, (j + 1) * BANK)
                        last = split3(ps(st)[:, cs], wh, wl, xh[:, b, cs], xl[:, b, cs], True, True)
                    last.then_inc(full["A"], 1)
                elif kind == "down":
                    r, b, s = a
                    e, c = divmod(s, HC)
                    g = expert_no(r, b, e)
                    k = blocks_before(r, b) * E * HC + s
                    pe.wait_ge(hl_ready, k + 1)
                    if r == FFN2 and b == 0 and s == 0:
                        pe.wait_ge(kvd_ready, NB)
                    wh = Wh[:, e, 1, c * P:(c + 1) * P]
                    wl = Wl[:, e, 1, c * P:(c + 1) * P]
                    for j in range(2):
                        cs = slice(j * BANK, (j + 1) * BANK)
                        if c == 0 and g > 0:
                            pe.wait_ge(b_free, 2 * (g - 1) + j + 1)
                        last = split3(psB[:, j, :], wh, wl, hh[:, slot(k), cs], hl[:, slot(k), cs], c == 0, c == HC - 1)
                        if c == HC - 1 and j == 0:
                            last.then_inc(b_full, 1)
                    last.then_inc(down_done, 1)
                elif kind == "accT":
                    r, b, ring = a
                    pe.wait_ge(acc_added, (blocks_before(r, b) + 1) * E)
                    for t in range(TB):
                        last = nc.tensor.transpose(ps(st)[:, t * P:(t + 1) * P], acc[:, b, t * P:(t + 1) * P], ident[:, :])
                    last.then_inc(full[ring], 1)
                elif kind in ("K", "V"):
                    n, i = a
                    if kind == "K" and i == 0 and n % 2 == 0:
                        b = n // 2
                        pe.wait_ge(xT_ready, xT_place(ATT, b) + 1)
                        pe.wait_ge(w_ready, WU)
                    ts_ = slice((ST * (n % 2) + i) * P, (ST * (n % 2) + i + 1) * P)
                    u = 1 if kind == "K" else 2
                    for j in range(2):
                        cs = slice(j * BANK, (j + 1) * BANK)
                        last = split3(ps(st)[:, cs], xh[:, n // 2, ts_], xl[:, n // 2, ts_], Ah[:, u, cs], Al[:, u, cs], True, True)
                    last.then_inc(full["A"], 1)
                elif kind == "Q":
                    n, j = a
                    cs = slice((n % 2) * BANK, (n % 2 + 1) * BANK)
                    for q in range(2):
                        c = 2 * j + q
                        last = split3(ps(st)[:, q * BANK:(q + 1) * BANK], Ah[:, 0, c * P:(c + 1) * P], Al[:, 0, c * P:(c + 1) * P],
                                      xh[:, n // 2, cs], xl[:, n // 2, cs], True, True)
                    last.then_inc(full["A"], 1)
                elif kind == "kv":
                    n, i = a
                    ti = ST * n + i
                    pe.wait_ge(feature_ready, feature_use[("K", n, i)] + 1)
                    pe.wait_ge(v_ready, ti + 1)
                    if i == 0 and n == 0:
                        pe.wait_ge(b_free, 2 * 2 * E)
                        wait_left(pe, last_c)
                    if i == 0 and n > 0:
                        pe.wait_ge(kvd_ready, n)
                        pe.wait_ge(den_read, 2 * n - 1)
                    for c in range(HP):
                        last = nc.tensor.matmul(kv_ps(c), km[:, ti % 2, c * P:(c + 1) * P], vt[:, ti % 2, c, :],
                                                start=(i == 0 and c % 3 == 0), stop=(i == ST - 1), skip_group_check=True)
                    last.then_inc(kv_done, 1)
                elif kind == "kvT":
                    n, = a
                    pe.wait_ge(kvd_ready, n + 1)
                    for c in range(HP):
                        last = nc.tensor.transpose(ps(st)[:, c * P:(c + 1) * P], kvd[:, c, :], ident[:, :])
                    last.then_inc(full["A"], 1)
                elif kind == "G":
                    n, = a
                    pe.wait_ge(kvT_ready, n + 1)
                    pe.wait_ge(att_loaded, 48)
                    for c in range(HP):
                        last = nc.tensor.matmul(ps(st)[:, c * P:(c + 1) * P], kvTs[:, c, :], wo_sb[:, c, :], start=True, stop=True)
                    last.then_inc(full["A"], 1)
                elif kind == "den":
                    n, hf = a
                    pe.wait_ge(kvd_ready, n + 1)
                    pe.wait_ge(feature_ready, feature_use[("Q", n, 3)] + 1)
                    if hf == 1 and n > 0:
                        pe.wait_ge(oT_ready, n)
                    for c in range(HP):
                        last = nc.tensor.matmul(den_ps(hf), ksum[:, 16 * c:16 * (c + 1)],
                                                qm[:, c, hf * BANK // 2:(hf + 1) * BANK // 2],
                                                start=(c == 0), stop=(c == HP - 1))
                    last.then_inc(den_full, 1)
                elif kind == "z":
                    n, j = a
                    pe.wait_ge(z_ready, n + 1)
                    for q in range(2):
                        c = 2 * j + q
                        last = nc.tensor.matmul(ps(st)[:, q * BANK:(q + 1) * BANK], pick[:, c, :], z2[:, :], start=True, stop=True)
                    last.then_inc(full["A"], 1)
                elif kind == "out":
                    n, j = a
                    pe.wait_ge(qz_ready, HP // 2 * n + j + 1)
                    pe.wait_ge(G_ready, n + 1)
                    if j == 0:
                        pe.wait_ge(den_read, 2 * (n + 1))
                    for c in (2 * j, 2 * j + 1):
                        last = nc.tensor.matmul(psC[:, 1, :], Gs[:, c, :], qm[:, c, :], start=(c == 0), stop=(c == HP - 1))
                    last.then_inc(out_done, 1)
                elif kind == "oT":
                    n, = a
                    pe.wait_ge(oT_ready, n + 1)
                    for t in range(ST):
                        last = nc.tensor.transpose(ps(st)[:, t * P:(t + 1) * P], oT[:, t * P:(t + 1) * P], ident[:, :])
                    last.then_inc(full["A"], 1)

        @block.scalar
        def _(act):
            for st in steps:
                kind, a = st[0], st[1:]
                if kind == "W0":
                    act.wait_ge(stage_loaded[0], 32)
                    nc.scalar.copy(Wh[:, 0, :, :], stage[:, 0, :, :]).then_inc(hi_split, 1)
                elif kind == "bias":
                    wait_full(act, st)
                    nc.scalar.copy(cols[:, :], ps(st)[:, 0:49]).then_inc(cols_ready, 1)
                elif kind == "xT":
                    r, b, ring = a
                    wait_full(act, st)
                    if r == ATT:
                        act.wait_ge(full["A"], last_use(("up", FFN1, b)))
                    if r == FFN2:
                        m = 2 * b + 1
                        act.wait_ge(full["A"], last_use(("K", m), ("V", m), ("Q", m)))
                    nc.scalar.copy(xh[:, b, :], ps(st)).then_inc(xh_ready, 1)
                elif kind == "probs":
                    act.wait_ge(logits_ready, place[st] + 1)
                    nc.scalar.activation(gX[:, :, :], gB[:, :, :], ACT.Exp, scale=1.0 / TEMP).then_inc(exp_ready, 1)
                elif kind == "up":
                    r, b, s = a
                    k = blocks_before(r, b) * E * HC + s
                    if k == 0:
                        act.wait_ge(cols_ready, 1)
                        act.wait_ge(consts_ready, 1)
                    if r == FFN2 and b == 0 and s == 0:
                        act.wait_ge(feature_ready, len(feature_use))
                        act.wait_ge(kv_done, NB * ST)
                    wait_full(act, st)
                    if k >= HS:
                        act.wait_ge(down_done, k - HS + 1)
                    if k >= 2:
                        act.wait_ge(hl_ready, k - 1)
                    bias = cols[:, s:s + 1]
                    nc.scalar.activation(hh[:, slot(k), :], ps(st), ACT.Gelu, bias=bias)
                    nc.scalar.activation(hid[:, k % 2, :], ps(st), ACT.Gelu, bias=bias).then_inc(hid_ready, 1)
                elif kind == "accT":
                    r, b, ring = a
                    wait_full(act, st)
                    earlier = [s2 for s2 in steps[:at[st]] if s2[0] == "xT"]
                    act.wait_ge(full[ring_use[earlier[-1]][0]], ring_use[earlier[-1]][1] + 1)
                    if place[st]:
                        act.wait_ge(x_ready, x_writes[[s2 for s2 in steps[:at[st]] if s2[0] == "addin"][-1]])
                    nc.scalar.copy(tok[:, :, :].rearrange("p t d -> p (t d)"), ps(st)).then_inc(acc_in_tok, 1)
                elif kind == "K":
                    n, i = a
                    k = feature_use[st]
                    act.wait_ge(R_ready, ST * n + i + 1)
                    if k == 0:
                        act.wait_ge(down_done, 2 * E * HC)
                        act.wait_ge(hl_ready, 2 * E * HC)
                    if k >= 2:
                        act.wait_ge(feature_ready, k - 1)
                    nc.scalar.activation(X[:, k % 2, :], R[:, k % 2, :], ACT.Exp)
                    nc.scalar.activation(R[:, k % 2, :], R[:, k % 2, :], ACT.Relu).then_inc(X_ready, 1)
                elif kind == "Q":
                    n, j = a
                    k = feature_use[st]
                    wait_full(act, st)
                    act.wait_ge(feature_ready, k - 1)
                    for q in range(2):
                        cs = slice(q * BANK, (q + 1) * BANK)
                        bias = cols[:, 40 + 2 * j + q:41 + 2 * j + q]
                        nc.scalar.activation(X[:, k % 2, cs], ps(st)[:, cs], ACT.Exp, bias=bias)
                        last = nc.scalar.activation(R[:, k % 2, cs], ps(st)[:, cs], ACT.Relu, bias=bias)
                    last.then_inc(X_ready, 1)
                elif kind == "kvout":
                    n, = a
                    act.wait_ge(kv_done, ST * (n + 1))
                    act.wait_ge(consts_ready, 1)
                    if n > 0:
                        act.wait_ge(den_full, 2 * n)
                        act.wait_ge(kvT_ready, n)
                    for hf in range(2):
                        ps_ = slice(64 * hf, 64 * hf + 64)
                        B3 = psB[ps_, :, 0:3 * (P + 1)].rearrange("p a (c m) -> p a c m", c=3)
                        C2 = psC[ps_, 0, 0:2 * (P + 1)].rearrange("p (c m) -> p c m", c=2)
                        cs = slice(64 * hf, 64 * hf + 64)
                        nc.scalar.copy(kvd[ps_, 0:6, cs].rearrange("p (a c) m -> p a c m", a=2), B3[:, :, :, cs])
                        nc.scalar.copy(kvd[ps_, 6:8, cs], C2[:, :, cs])
                        nc.scalar.copy(ksum[ps_, hf:hf + 91:18].rearrange("p (a c) -> p a c", a=2), B3[:, :, :, P])
                        last = nc.scalar.copy(ksum[ps_, 108 + hf:108 + hf + 19:18], C2[:, :, P])
                    last.then_inc(kvd_ready, 1)
                elif kind == "kvT":
                    n, = a
                    wait_full(act, st)
                    if n == 0:
                        act.wait_ge(b_free, 2 * 2 * E)
                    nc.scalar.copy(kvTs[:, :, :].rearrange("p c m -> p (c m)"), ps(st)).then_inc(kvT_ready, 1)
                elif kind == "G":
                    n, = a
                    wait_full(act, st)
                    if n > 0:
                        act.wait_ge(out_done, HP // 2 * n)
                    nc.scalar.copy(Gs[:, :, :].rearrange("p c m -> p (c m)"), ps(st)).then_inc(G_ready, 1)
                elif kind == "outc":
                    n, = a
                    act.wait_ge(out_done, HP // 2 * (n + 1))
                    if n > 0:
                        act.wait_ge(full["A"], ring_use[("oT", n - 1)][1] + 1)
                    nc.scalar.activation(oT[:, :], psC[:, 1, :], ACT.Identity, bias=cols[:, 48:49]).then_inc(oT_ready, 1)

        @block.vector
        def _(dve):
            link_count = [0]

            def link(ins):
                link_count[0] += 1
                ins.then_inc(dve_chain, 1)
                dve.wait_ge(dve_chain, link_count[0])

            def block_stats(src):
                for t in range(TB):
                    last = nc.vector.bn_stats(bst[:, t, :], src(t))
                link(last)
                for t in range(TB):
                    last = nc.vector.bn_aggr(mv[:, t, :], bst[:, t, :])
                last.then_inc(stats_ready, 1)

            def bc(v):
                return v.unsqueeze(2).to_broadcast([P, TB, E])

            for st in steps:
                kind, a = st[0], st[1:]
                if kind == "W" and a[0] == 0:
                    nc.vector.memset(z2[:, :].bitcast(F32), 0.0)
                    dve.wait_ge(small_loaded, 32)
                    link(nc.vector.tensor_copy(gwh[:, :], gw[:, :]))
                    nc.vector.tensor_tensor(gwl[:, :], gw[:, :], gwh[:, :].bitcast(F32), ALU.subtract).then_inc(gw_ready, 2)
                elif kind == "stats":
                    r, b = a
                    if r == FFN1:
                        dve.wait_ge(x_loaded[b], 16)
                    else:
                        dve.wait_ge(x_ready, x_writes[x_parts(r, b)])
                    block_stats(lambda t: x[:, b * TB + t, :])
                elif kind == "W0":
                    dve.wait_ge(hi_split, 1)
                    nc.vector.tensor_tensor(Wl[:, 0, :, :], stage[:, 0, :, :], Wh[:, 0, :, :].bitcast(F32),
                                            ALU.subtract).then_inc(w_ready, 1)
                elif kind == "norm":
                    r, b = a
                    dve.wait_ge(rstd_ready, place[("stats", r, b)] + 1 + sum(s2[0] == "accT" for s2 in steps[:at[("stats", r, b)]]))
                    earlier = [s2 for s2 in steps[:at[st]] if s2[0] == "xT"]
                    if earlier:
                        dve.wait_ge(full[ring_use[earlier[-1]][0]], ring_use[earlier[-1]][1] + 1)
                    for t in range(TB):
                        last = nc.vector.tensor_scalar(tok[:, t, :], x[:, b * TB + t, :], mv[:, t, 0:1], rstd[:, t:t + 1],
                                                       ALU.subtract, ALU.mult)
                    last.then_inc(tok_ready, 1)
                elif kind == "xT":
                    r, b, ring = a
                    dve.wait_ge(xh_ready, place[st] + 1)
                    nc.vector.tensor_tensor(xl[:, b, :], ps(st), xh[:, b, :].bitcast(F32), ALU.subtract).then_inc(xT_ready, 1)
                elif kind == "gate":
                    wait_full(dve, st)
                    nc.vector.tensor_tensor(gL[:, :, :], ps(st)[:, 0:TB * E].rearrange("p (t e) -> p t e", t=TB),
                                            gb[:, :].unsqueeze(1).to_broadcast([P, TB, E]), ALU.add).then_inc(logits_read, 1)
                    dve.wait_ge(logits_read, place[st] + 1)
                    link(nc.vector.tensor_reduce(gm1[:, :], gL[:, :, :], AX_X, ALU.max))
                elif kind == "rank":
                    i = a[2]
                    rank = order[:, :].unsqueeze(1).to_broadcast([P, TB, E])
                    best = gm1 if i == 0 else gm2
                    if i in (0, 2):
                        link(nc.vector.tensor_tensor(gA[:, :, :], gL[:, :, :] if i == 0 else gX[:, :, :], bc(best[:, :]), ALU.is_equal))
                        link(nc.vector.tensor_tensor(gA[:, :, :], gA[:, :, :], rank, ALU.mult))
                        link(nc.vector.tensor_reduce(gm2[:, :], gA[:, :, :], AX_X, ALU.max))
                    elif i == 1:
                        link(nc.vector.tensor_tensor(gS[:, :, :], gA[:, :, :], bc(gm2[:, :]), ALU.is_equal))
                        link(nc.vector.scalar_tensor_tensor(gX[:, :, :], gS[:, :, :], FAR, gL[:, :, :], ALU.mult, ALU.add))
                        link(nc.vector.tensor_reduce(gm2[:, :], gX[:, :, :], AX_X, ALU.max))
                    else:
                        link(nc.vector.tensor_tensor(gA[:, :, :], gA[:, :, :], bc(gm2[:, :]), ALU.is_equal))
                        link(nc.vector.tensor_tensor(gS[:, :, :], gS[:, :, :], gA[:, :, :], ALU.add))
                        nc.vector.tensor_tensor(gB[:, :, :], gL[:, :, :], bc(gm1[:, :]), ALU.subtract).then_inc(logits_ready, 1)
                elif kind == "probs":
                    dve.wait_ge(exp_ready, place[st] + 1)
                    link(nc.vector.tensor_tensor(gA[:, :, :], gX[:, :, :], gS[:, :, :], ALU.mult))
                    link(nc.vector.tensor_reduce(gsum[:, :], gA[:, :, :], AX_X, ALU.add))
                    link(nc.vector.reciprocal(gsum[:, :], gsum[:, :]))
                    nc.vector.tensor_tensor(probs[:, :, :].rearrange("p e t -> p t e"), gA[:, :, :], bc(gsum[:, :]),
                                            ALU.mult).then_inc(probs_ready, 1)
                elif kind == "probsT":
                    wait_full(dve, st)
                    if place[st]:
                        dve.wait_ge(table_stored, 16 * place[st])
                    nc.vector.tensor_copy(pT[:, :], ps(st)[0:E * TB, 0:P]).then_inc(pT_ready, 1)
                elif kind == "low":
                    r, b, s = a
                    k = blocks_before(r, b) * E * HC + s
                    dve.wait_ge(hid_ready, k + 1)
                    if k >= HS:
                        dve.wait_ge(down_done, k - HS + 1)
                    if r == FFN2 and b == 0 and s < HS:
                        dve.wait_ge(kv_done, NB * ST)
                        if s:
                            dve.wait_ge(out_done, (NB - 1) * HP // 2 + s)
                    nc.vector.tensor_tensor(hl[:, slot(k), :], hid[:, k % 2, :], hh[:, slot(k), :].bitcast(F32),
                                            ALU.subtract).then_inc(hl_ready, 1)
                elif kind == "down" and a[2] % HC == HC - 1:
                    r, b, s = a
                    e = s // HC
                    g = expert_no(r, b, e)
                    k = blocks_before(r, b) * E * HC + s
                    dve.wait_ge(pb_loaded[g % 2], 16 * (g // 2 + 1))
                    if e == 0 and (r, b) != (FFN1, 0) and (r, b) != (FFN1, 1):
                        pr = ("accT", FFN1, b, "A" if b else "C")
                        dve.wait_ge(full[pr[3]], ring_use[pr][1] + 1)
                    if (r, b, e) == (FFN2, 0, 0):
                        dve.wait_ge(out_done, NB * HP // 2)
                    if g >= 2:
                        dve.wait_ge(acc_added, g - 1)
                    for j in range(2):
                        cs = slice(j * BANK, (j + 1) * BANK)
                        if j == 0:
                            dve.wait_ge(b_full, g + 1)
                        else:
                            dve.wait_ge(down_done, k + 1)
                        dst = acc[:, b, cs] if e == 0 else gated[:, g % 2, cs]
                        last = nc.vector.scalar_tensor_tensor(dst, psB[:, j, :], cols[:, 32 + e:33 + e], pb[:, g % 2, cs],
                                                              ALU.add, ALU.mult)
                        last.then_inc(b_free, 1)
                elif kind == "accT":
                    r, b, ring = a
                    dve.wait_ge(acc_in_tok, place[st] + 1)
                    block_stats(lambda t: tok[:, t, :])
                elif kind == "addin":
                    r, b = a
                    me = [s2 for s2 in steps if s2[0] == "accT" and s2[1:3] == (r, b)][0]
                    dve.wait_ge(rstd_ready, 1 + sum(s2[0] in ("accT", "stats") for s2 in steps[:at[me]]))
                    for t in range(TB):
                        last = nc.vector.tensor_scalar(tok[:, t, :], tok[:, t, :], mv[:, t, 0:1], rstd[:, t:t + 1],
                                                       ALU.subtract, ALU.mult)
                    link(last)
                    link(nc.vector.tensor_tensor(tok[:, :, :], tok[:, :, :], gain[:, :].unsqueeze(1).to_broadcast([P, TB, P]),
                                                 ALU.mult))
                    xb = x[:, b * TB:(b + 1) * TB, :]
                    dve.wait_ge(x_shifted, blocks_before(r, b) + 1)
                    nc.vector.tensor_tensor(xb, xb, tok[:, :, :], ALU.add).then_inc(x_ready, 1)
                elif kind == "K":
                    n, i = a
                    k = feature_use[st]
                    wait_full(dve, st)
                    if k == 0:
                        dve.wait_ge(down_done, 2 * E * HC)
                        dve.wait_ge(att_loaded, 48)
                    if k >= 2:
                        dve.wait_ge(feature_ready, k - 1)
                    nc.vector.tensor_tensor(R[:, k % 2, :], ps(st), bkv[:, 0, :], ALU.add).then_inc(R_ready, 1)
                elif kind == "V":
                    n, i = a
                    ti = ST * n + i
                    wait_full(dve, st)
                    if ti >= 2:
                        dve.wait_ge(kv_done, ti - 1)
                    nc.vector.tensor_tensor(vt[:, ti % 2, :, 0:P], ps(st).rearrange("p (c m) -> p c m", c=HP),
                                            bkv[:, 1, :].rearrange("p (c m) -> p c m", c=HP), ALU.add).then_inc(v_ready, 1)
                elif kind in ("Kf", "Qf"):
                    n, i = a
                    k = feature_use[(kind[0], n, i)]
                    dve.wait_ge(X_ready, k + 1)
                    if kind == "Kf":
                        ti = ST * n + i
                        if ti == 0:
                            dve.wait_ge(hl_ready, 2 * E * HC)
                        if ti >= 2:
                            dve.wait_ge(kv_done, ti - 1)
                        dst = km[:, ti % 2, :]
                    else:
                        if n == 0 and i == 0:
                            dve.wait_ge(acc_added, 2 * E)
                        if n > 0:
                            dve.wait_ge(out_done, HP // 2 * (n - 1) + i + 1)
                        dst = qm[:, 2 * i:2 * i + 2, :].rearrange("p c n -> p (c n)")
                    nc.vector.scalar_tensor_tensor(dst, X[:, k % 2, :], 1.0, R[:, k % 2, :], ALU.min, ALU.add)\
                        .then_inc(feature_ready, 1)
                elif kind == "denz":
                    n, hf = a
                    if hf == 0 and n > 0:
                        dve.wait_ge(full["A"], ring_use[("oT", n - 1)][1] + 1)
                    dve.wait_ge(den_full, 2 * n + hf + 1)
                    cs = slice(hf * BANK // 2, (hf + 1) * BANK // 2)
                    nc.vector.tensor_scalar(zr[:, cs], den_ps(hf), ATT_EPS, None, ALU.add).then_inc(den_read, 1)
                    dve.wait_ge(den_read, 2 * n + hf + 1)
                    link(nc.vector.reciprocal(zr[:, cs], zr[:, cs]))
                    if hf == 0 and n > 0:
                        dve.wait_ge(full["A"], ring_use[("z", n - 1, 3)][1] + 1)
                    link(nc.vector.tensor_copy(z2[0:16, cs], zr[:, cs]))
                    last = nc.vector.tensor_tensor(z2[32:48, cs], zr[:, cs], z2[0:16, cs].bitcast(F32), ALU.subtract)
                    if hf == 1:
                        last.then_inc(z_ready, 1)
                elif kind == "z":
                    n, j = a
                    wait_full(dve, st)
                    q2 = qm[:, 2 * j:2 * j + 2, :].rearrange("p c n -> p (c n)")
                    nc.vector.tensor_tensor(q2, q2, ps(st), ALU.mult).then_inc(qz_ready, 1)
                elif kind == "oT":
                    n, = a
                    wait_full(dve, st)
                    xb = x[:, ST * n:ST * (n + 1), :]
                    nc.vector.tensor_tensor(xb, xb, ps(st)[:, 0:BANK].rearrange("p (t d) -> p t d", t=ST),
                                            ALU.add).then_inc(x_ready, 1)

        @block.gpsimd
        def _(pool):
            link_count = [0]

            def link(ins):
                link_count[0] += 1
                ins.then_inc(pool_chain, 1)
                pool.wait_ge(pool_chain, link_count[0])

            link(nc.gpsimd.memset(ident[:, :], 0.0))
            link(nc.gpsimd.affine_select(out=ident[:, :], in_=ident[:, :], compare_op=ALU.not_equal, fill=1.0, base=0,
                                         pattern=[[-1, P]], channel_multiplier=1))
            nc.gpsimd.memset(half[:, :], -0.5)
            link(nc.gpsimd.memset(hid[0:48, 0, :], 0.0))
            for row in (0, 32):
                v = hid[0:48, 0, :].rearrange("k (c j m) -> k c j m", c=HP, j=2)
                link(nc.gpsimd.affine_select(out=v, in_=v, compare_op=ALU.not_equal, fill=1.0, base=-row,
                                             pattern=[[-2, HP], [-1, 2], [0, P // 2]], channel_multiplier=1))
            nc.gpsimd.tensor_copy(pick[:, :, :].rearrange("k c m -> k (c m)"), hid[0:48, 0, :])
            for e in range(E):
                nc.gpsimd.memset(order[:, e:e + 1], float(E - e))
            nc.gpsimd.memset(vt[:, :, :, P:P + 1], 1.0)
            nc.gpsimd.memset(ksum[:, :], 0.0)
            nc.gpsimd.memset(kvd[:, :, :], 0.0).then_inc(consts_ready, 1)
            for st in steps:
                kind, a = st[0], st[1:]
                if kind in ("stats", "accT"):
                    n = sum(s2[0] in ("accT", "stats") for s2 in steps[:at[st]])
                    pool.wait_ge(stats_ready, n + 1)
                    link(nc.gpsimd.tensor_scalar(ve[:, :], mv[:, :, 1], LN_EPS, 1.0, ALU.add, ALU.mult))
                    nc.gpsimd.tensor_tensor(rstd[:, :], ve[:, :], half[:, :], ALU.pow).then_inc(rstd_ready, 1)
                    if kind == "stats" and st[1:] == (FFN1, 0):
                        pool.wait_ge(ln_loaded, 32)
                        link(nc.gpsimd.tensor_scalar(gain[:, :], gain[:, :], 0.5, 1.0, ALU.mult, ALU.mult))
                        link(nc.gpsimd.tensor_scalar(shift[:, :], shift[:, :], 0.5, 1.0, ALU.mult, ALU.mult))
                if kind == "W" and a[0] > 0:
                    u, = a
                    pool.wait_ge(stage_loaded[u % 2], 32 * (u // 2 + 1))
                    s = stage[:, u % 2, :, :]
                    h, l = (Wh[:, u, :, :], Wl[:, u, :, :]) if u < E else (
                        Ah[:, u - E, :].rearrange("p (a n) -> p a n", a=2), Al[:, u - E, :].rearrange("p (a n) -> p a n", a=2))
                    link(nc.gpsimd.tensor_copy(h, s))
                    if u == 1:
                        pool.wait_ge(w_ready, 1)
                    nc.gpsimd.tensor_tensor(l, s, h.bitcast(F32), ALU.subtract).then_inc(w_ready, 1)
                elif kind == "norm" and a[0] != ATT:
                    r, b = a
                    pool.wait_ge(tok_ready, tok_writes[st])
                    xb = x[:, b * TB:(b + 1) * TB, :]
                    nc.gpsimd.tensor_tensor(xb, xb, shift[:, :].unsqueeze(1).to_broadcast([P, TB, P]), ALU.add)\
                        .then_inc(x_shifted, 1)
                elif kind == "down" and a[2] % HC == HC - 1:
                    r, b, s = a
                    e = s // HC
                    g = expert_no(r, b, e)
                    pool.wait_ge(b_free, 2 * (g + 1))
                    if g:
                        pool.wait_ge(acc_added, g)
                    if e == 0:
                        pool.engine_nop().then_inc(acc_added, 1)
                    else:
                        nc.gpsimd.tensor_tensor(acc[:, b, :], acc[:, b, :], gated[:, g % 2, :], ALU.add).then_inc(acc_added, 1)


_INS = ['L0_attn_x', 'L0_attn_wq', 'L0_attn_bq', 'L0_attn_wk', 'L0_attn_bk', 'L0_attn_wv', 'L0_attn_bv', 'L0_attn_wo',
        'L0_attn_bo', 'L0_ffn_gate_w', 'L0_ffn_gate_b', 'L0_ffn_w1', 'L0_ffn_b1', 'L0_ffn_w2', 'L0_ffn_b2',
        'L0_ffn_ln_g', 'L0_ffn_ln_b']
_OUTS = [((4, 512, 128), 'float32')]


def kernel(**inputs):
    import numpy as _np
    import concourse.bacc as _bacc
    from concourse import mybir as _mybir
    from concourse.bass_utils import run_bass_kernel_spmd as _run

    nc = _bacc.Bacc("TRN2", target_bir_lowering=False, num_devices=1)
    arrays, args = {}, []
    for name in _INS:
        a = _np.ascontiguousarray(inputs[name])
        arrays[f"in_{name}_dram"] = a
        args.append(nc.dram_tensor(f"in_{name}_dram", a.shape, _mybir.dt.from_np(a.dtype), kind="ExternalInput").ap())
    for i, (shape, dtype) in enumerate(_OUTS):
        dt = _mybir.dt.from_np(_np.dtype(dtype))
        args.append(nc.dram_tensor(f"out_{i}_dram", shape, dt, kind="ExternalOutput").ap())
    bass_macaron_kernel(nc, *args)
    r = _run(nc, [arrays], core_ids=[0])
    got = tuple(r.results[0][f"out_{i}_dram"] for i in range(len(_OUTS)))
    return got[0]
```

```python
from contextlib import ExitStack

import concourse.bass as bass
from concourse import mybir

ALU = mybir.AluOpType
ACT = mybir.ActivationFunctionType
F32 = mybir.dt.float32
F32R = mybir.dt.float32r
AX_X = mybir.AxisListType.X

P = 128
TILES = 16
TB = 8
BLK = TB * P
BANK = 512
HT = TB // 2
E = 8
HC = 4
HP = 8
NB = 4
ST = 4
WU = 10
TEMP = 0.9
LOG2_E = 1.4426950408889634
LN_EPS = 1e-5
ATT_EPS = 1e-6
FAR = -3.0e38
LAG = 2
HS = LAG + 1
WARM_UP = 12
LAST_CHUNK = 4 * E * HC - 1
FFN1, ATT, FFN2 = 0, 1, 2
NORMS_OF_DVE = ((FFN1, 0), (ATT, 0), (ATT, 1), (FFN2, 0))


FIRST = """Q.n.0 Kf.n.1 K.n.2 Qf.n.0 Kf.n.2 kv.n.0 Q.n.1 kv.n.1 K.n.3 Qf.n.1 Q.n.2 kv.n.2 Q.n.3 Kf.n.3 Qf.n.2"""
BATCH = """Qf.n.3 kv.n.3 kvout.n K.m.0 ksum.n oT.o x0 K.m.1 den.n.0 Kf.m.0 den.n.1 denz.n.0 x1 Kf.m.1
           K.m.2 kv.m.0 x2 denz.n.1 kv.m.1 K.m.3 Kf.m.2 G.n x3 Kf.m.3 Q.m.0 z.n.0 kv.m.2 x4 z.n.1 Q.m.1 out.n.0
           Qf.m.0 z.n.2 out.n.1 Qf.m.1 x5 Q.m.2 z.n.3 out.n.2 Qf.m.2 x6 Q.m.3 out.n.3 x7 outc.n"""
LAST = """kv.n.3 ksum.n kvout.n Qf.n.3 oT.o up.0 low.0 den.n.0 denz.n.0 den.n.1 up.1 denz.n.1 G.n down.0
          z.n.0 z.n.1 out.n.0 z.n.2 out.n.1 z.n.3 low.1 up.2 out.n.2 probsT out.n.3 outc.n low.2"""
EXTRA = {(0, 0): [("accT", FFN1, 1, "A"), ("stats2", FFN1, 1, 1)],
         (0, 2): [("addin", FFN1, 1, q) for q in range(4)],
         (0, 5): [("stats", ATT, 1), ("stats2", ATT, 1)],
         (0, 7): [("norm", ATT, 1), ("xT", ATT, 1, "A")],
         (2, 0): [("stats", FFN2, 0), ("stats2", FFN2, 0)],
         (2, 3): [("norm", FFN2, 0)],
         (2, 4): [("xT", FFN2, 0, "A")],
         (2, 5): [("gate", FFN2, 0, "A")],
         (2, 6): [("gateT", FFN2, 0, "A"), *(("rank", FFN2, 0, i) for i in range(4)), ("probs", FFN2, 0)]}


def timeline():
    t = []

    def steps_of(words, n, extra={}):
        batch = {"o": n - 1, "n": n, "m": n + 1}
        for word in words.split():
            kind, *a = word.split(".")
            if kind[0] == "x":
                t.extend(extra.get((n, int(kind[1:])), ()))
            elif kind in ("up", "low", "down"):
                t.append((kind, FFN2, 0, int(a[0])))
            elif kind == "probsT":
                t.append((kind, FFN2, 0, "A"))
            elif batch[a[0]] >= 0:
                t.append((kind, batch[a[0]], *(int(v) for v in a[1:])))

    def ffn(r, between, first=0):
        for k in range(first, 2 * E * HC):
            b, s = divmod(k, E * HC)
            t.append(("up", r, b, s))
            t.extend(between.get((b, s), ()))
            if k >= LAG:
                t.append(("down", r, *divmod(k - LAG, E * HC)))
            t.append(("low", r, b, s))

    t += [("W", 0), ("stats", FFN1, 0), ("stats2", FFN1, 0), ("norm", FFN1, 0), ("W0", 0), ("xT", FFN1, 0, "C"), ("bias",), ("W0", 1)]
    between = {(0, HC * e + 2): [("W", e + 2)] for e in range(E)}

    def insert(where, *sts):
        between.setdefault(where, []).extend(sts)

    insert((0, 0), ("gate", FFN1, 0, "C"))
    insert((0, 1), ("gateT", FFN1, 0, "C"), *(("rank", FFN1, 0, i) for i in range(4)), ("W", 1))
    insert((0, 2), ("probs", FFN1, 0))
    insert((0, 3), ("probsT", FFN1, 0, "C"))
    insert((0, 6), ("stats", FFN1, 1))
    insert((0, 7), ("stats2", FFN1, 1), ("norm", FFN1, 1))
    insert((0, 15), ("xT", FFN1, 1, "C"))
    insert((0, 18), ("gate", FFN1, 1, "C"))
    insert((0, 19), ("gateT", FFN1, 1, "C"))
    for i in range(4):
        insert((0, (20, 22, 23, 24)[i]), ("rank", FFN1, 1, i))
    insert((0, 26), ("probs", FFN1, 1))
    insert((0, 29), ("probsT", FFN1, 1, "C"))
    insert((0, 26), ("consts",))
    insert((0, 31), ("W", WU), ("prep", 0))
    insert((1, 2), ("prep", 1))
    insert((1, 4), ("prep", 2))
    insert((1, 6), ("accT", FFN1, 0, "C"))
    insert((1, 7), ("stats2", FFN1, 0, 1))
    for q in range(4):
        insert((1, 8 + q), ("addin", FFN1, 0, q))
    insert((1, 8), ("bvwo", "C"))
    insert((1, 10), ("wvT", "C"), ("kbias",))
    insert((1, 12), ("VW", 0, "C"))
    insert((1, 14), ("VW", 1, "C"))
    insert((1, 18), ("stats", ATT, 0))
    insert((1, 19), ("stats2", ATT, 0), ("norm", ATT, 0))
    insert((1, 26), ("xT", ATT, 0, "C"))
    ffn(FFN1, between)

    b_last = E * HC - 1
    t += [("K", 0, 0), ("down", FFN1, 1, b_last - 1), ("K", 0, 1), ("down", FFN1, 1, b_last),
          ("Kf", 0, 0)]
    steps_of(FIRST, 0)
    for n in range(NB - 1):
        steps_of(BATCH, n, EXTRA)

    n = NB - 1
    steps_of(LAST, n)

    between = {}
    insert((0, 3), ("oT", n))
    insert((0, 6), ("stats", FFN2, 1))
    insert((0, 7), ("stats2", FFN2, 1), ("norm", FFN2, 1))
    insert((0, 11), ("xT", FFN2, 1, "C"))
    insert((0, 13), ("gate", FFN2, 1, "C"))
    insert((0, 14), ("gateT", FFN2, 1, "C"))
    for i in range(4):
        insert((0, (15, 16, 18, 19)[i]), ("rank", FFN2, 1, i))
    insert((0, 20), ("probs", FFN2, 1))
    insert((0, 23), ("probsT", FFN2, 1, "C"))
    insert((1, 6), ("accT", FFN2, 0, "C"))
    insert((1, 7), ("stats2", FFN2, 0, 1))
    insert((1, 18), ("store",))
    for q in range(4):
        insert((1, 8 + q), ("addin", FFN2, 0, q))
    ffn(FFN2, between, 3)
    t += [("down", FFN2, 1, b_last - 1), ("down", FFN2, 1, b_last), ("accT", FFN2, 1, "C")]
    return t


def bass_macaron_kernel(nc: bass.Bass, x_in, wq, bq, wk, bk, wv, bv, wo, bo, gate_w, gate_b,
                        w1, b1, w2, b2, ln_g, ln_b, out):
    steps = timeline()

    place, ring_use, uses, kinds = {}, {}, {"A": 0, "C": 0}, {}
    feature_use = {}
    for st in steps:
        k = st[0]
        place[st] = kinds.get(k, 0)
        kinds[k] = place[st] + 1
        ring = st[-1] if st[-1] in ("A", "C") else (
            "A" if k in ("bias", "up", "K", "Q", "G", "z", "oT") else None)
        if ring:
            ring_use[st] = (ring, uses[ring])
            uses[ring] += 1
        if k in ("K", "Q"):
            feature_use[st] = len(feature_use)
    at = {st: i for i, st in enumerate(steps)}
    c_uses_before_attention = sum(1 for st, (r, _) in ring_use.items() if r == "C" and at[st] < at[("K", 0, 0)])

    ctx = ExitStack()
    with ctx:
        def sb(name, shape, dt=F32, scope=ctx):
            return scope.enter_context(nc.sbuf_tensor(name, shape, dt))

        def sem(name):
            return ctx.enter_context(nc.semaphore(name))

        x = sb("x", [P, TILES, P])
        xh = sb("xh", [P, 2, BLK], F32R)
        xl = sb("xl", [P, 2, BLK], F32R)
        Wh = sb("Wh", [P, E, 2, BANK], F32R)
        Wl = sb("Wl", [P, E, 2, BANK], F32R)
        Ah = sb("Ah", [P, 2, 2 * BANK], F32R)
        Al = sb("Al", [P, 2, 2 * BANK], F32R)
        wo_sb = sb("wo_sb", [P, HP, P])
        VW = sb("VW", [P, HP, 2 * P])
        stage = sb("stage", [P, 2, 2, BANK])
        bk1 = stage[:, 0, :, :].rearrange("p a n -> p (a n)")
        bvwo = stage[:, 1, :, :].rearrange("p a (c m) -> p (a c) m", m=P)
        acc = sb("acc", [P, 2, BLK])
        xn = sb("xn", [P, TILES, P])
        kt = sb("kt", [P, HP, P])
        kcol = sb("kcol", [P, HP])
        ksum = sb("ksum", [P, HP * 16])
        tok = sb("tok", [P, TB, P])
        wo2 = xn[:, :, :].rearrange("p t m -> p (t m)").rearrange("p (c m) -> p c m", c=HP)
        gT = tok[0:2 * E, :, :].rearrange("e t p -> e (t p)")
        ident = sb("ident", [P, P])
        pick = sb("pick", [48, HP, P], F32R)
        gain = sb("gain", [P, P])
        shift = sb("shift", [P, P])
        rows = sb("rows", [57, P])
        cols = sb("cols", [P, 57])
        gw = sb("gw", [P, E])
        gw2 = sb("gw2", [P, 2 * E], F32R)
        gb = sb("gb", [P, E])
        order = sb("order", [P, E])
        ones = sb("ones", [P, 1])
        less1 = sb("less1", [P, 1])
        warm = sb("warm", [P, 1])
        half = sb("half", [P, TB])
        bst = sb("bst", [P, TB, 6])
        mv = sb("mv", [P, TB, 2])
        ve = sb("ve", [P, TB])
        rstd = sb("rstd", [P, TB])
        gL = sb("gL", [P, TB, E])
        gA = sb("gA", [P, TB, E])
        gS = sb("gS", [P, TB, E])
        gX = sb("gX", [P, TB, E])
        gm1 = sb("gm1", [P, TB])
        gm2 = sb("gm2", [P, TB])
        g2nd = sb("g2nd", [P, TB])
        two = sb("two", [P, TB])
        gsum = sb("gsum", [P, TB])
        probs = sb("probs", [P, E, TB])
        pT = sb("pT", [E * TB, P])

        ffn_only = ExitStack()
        pb = sb("pb", [P, 2, BLK], scope=ffn_only)
        hh = sb("hh", [P, HS, BLK], F32R, scope=ffn_only)
        hid = sb("hid", [P, 2, BLK], scope=ffn_only)
        hl = sb("hl", [P, HS, BLK], F32R, scope=ffn_only)
        gated = sb("gated", [P, 2, BLK], scope=ffn_only)
        ffn_only.close()
        kxT = sb("kxT", [P, HP, P])
        Gs = sb("Gs", [P, HP, P])
        R = sb("R", [P, 2, 2 * BANK])
        X = sb("X", [P, 2, 2 * BANK])
        km = sb("km", [P, 2, 2 * BANK])
        qm = sb("qm", [P, HP, BANK])
        z2 = sb("z2", [48, BANK], F32R)
        oT = acc[:, 0, 0:BANK]
        zr = oT[0:16, :]

        psA = ctx.enter_context(nc.psum_tensor("psA", [P, 2, 2 * BANK], F32))
        psB = ctx.enter_context(nc.psum_tensor("psB", [P, 2, BANK], F32))
        psC = ctx.enter_context(nc.psum_tensor("psC", [P, 2, BANK], F32))

        table = nc.dram_tensor("gate_table", [4, E * TB, P], F32, kind="Internal").ap()

        def ps(st):
            ring, n = ring_use[st]
            return psA[:, n % 2, :] if ring == "A" else psC[:, :, :].rearrange("p a n -> p (a n)")

        ksum_ps = psC[:, 0, BANK // 2:BANK // 2 + HP]

        def den_ps(hf):
            return psC[0:16, hf, 0:BANK // 2]

        x_loaded = [sem("x_loaded0"), sem("x_loaded1"), sem("x_loaded2")]
        small_loaded = sem("small_loaded")
        ln_loaded = sem("ln_loaded")
        rows_loaded = sem("rows_loaded")
        wo_loaded = sem("wo_loaded")
        bk_loaded = sem("bk_loaded")
        bk1_ready = sem("bk1_ready")
        stage_loaded = [sem("stage_loaded0"), sem("stage_loaded1")]
        w1_loaded = sem("w1_loaded")
        w2_loaded = sem("w2_loaded")
        table_stored = sem("table_stored")
        pb_loaded = [sem("pb_loaded0"), sem("pb_loaded1")]
        stored = sem("stored")
        ident_ready = sem("ident_ready")
        consts_ready = sem("consts_ready")
        hi_split = sem("hi_split")
        w1_ready = sem("w1_ready")
        w_ready = sem("w_ready")
        gw_ready = sem("gw_ready")
        cols_ready = sem("cols_ready")
        full = {"A": sem("fullA"), "C": sem("fullC")}
        half_full = sem("half_full")
        b_full = sem("b_full")
        b_free = sem("b_free")
        stats_ready = sem("stats_ready")
        rstd_ready = sem("rstd_ready")
        tok_ready = sem("tok_ready")
        x_shifted = sem("x_shifted")
        xh_ready = sem("xh_ready")
        xT_ready = sem("xT_ready")
        gT_ready = sem("gT_ready")
        logits_read = sem("logits_read")
        logits_ready = sem("logits_ready")
        exp_ready = sem("exp_ready")
        probs_ready = sem("probs_ready")
        pT_ready = sem("pT_ready")
        hid_ready = sem("hid_ready")
        hl_ready = sem("hl_ready")
        hid_half = sem("hid_half")
        hl_half = sem("hl_half")
        down_done = sem("down_done")
        gated_ready = sem("gated_ready")
        acc_added = sem("acc_added")
        acc_final = sem("acc_final")
        acc_half = sem("acc_half")
        acc_in_tok = sem("acc_in_tok")
        x_added = sem("x_added")
        att_added = sem("att_added")
        x_final = sem("x_final")
        R_ready = sem("R_ready")
        X_ready = sem("X_ready")
        feature_ready = sem("feature_ready")
        prep_ready = sem("prep_ready")
        fold_read = sem("fold_read")
        ksum_ready = sem("ksum_ready")
        bias_ready = sem("bias_ready")
        kv_done = sem("kv_done")
        kxT_ready = sem("kxT_ready")
        ksum_full = sem("ksum_full")
        kt_added = sem("kt_added")
        G_ready = sem("G_ready")
        den_full = sem("den_full")
        den_read = sem("den_read")
        z_ready = sem("z_ready")
        qz_ready = sem("qz_ready")
        out_done = sem("out_done")
        oT_ready = sem("oT_ready")
        dve_chain = sem("dve_chain")
        pool_chain = sem("pool_chain")

        def wait_full(eng, st):
            ring, n = ring_use[st]
            eng.wait_ge(full[ring], n + 1)

        def wait_left(eng, st):
            kind, a = st[0], st[1:]
            done, n = {
                "bias": (cols_ready, 1),
                "xT": (xT_ready, 2 * place[st] + 2),
                "gate": (gT_ready, place[st] + 1),
                "gateT": (logits_read, place[st] + 1),
                "probsT": (pT_ready, place[st] + 1),
                "up": (hid_ready, place[st] + 1),
                "accT": (acc_in_tok, place[st] + 1),
                "K": (R_ready, place[st] + 1),
                "bvwo": (fold_read, 1),
                "wvT": (fold_read, 2),
                "VW": (fold_read, 3 + place[st]),
                "Q": (X_ready, feature_use.get(st, 0) + 1),
                "G": (G_ready, place[st] + 1),
                "z": (qz_ready, place[st] + 1),
                "oT": (att_added, place[st] + 1),
            }[kind]
            eng.wait_ge(done, n)

        def wait_free(eng, st):
            ring, n = ring_use[st]
            slots = 2 if ring == "A" else 1
            if n >= slots:
                wait_left(eng, used_by[ring, n - slots])

        def wait_stage(eng, u):
            eng.wait_ge(stage_loaded[u % 2], 32 * (u // 2 + u % 2))

        def expert_no(r, b, e):
            return (2 * (r == FFN2) + b) * E + e

        def fslot(k):
            return (k + 1) % 2

        def adds_of(tile):
            return (ST - 1) * (tile // ST) + max(tile % ST, 1)

        def blocks_before(r, b):
            return 2 * (r == FFN2) + b

        def slot(k):
            return (k - 2 * E * HC) % HS

        def wait_x(eng, r, b, h):
            if r == FFN1:
                eng.wait_ge(x_loaded[h if b == 0 else 2], 16)
            elif r == ATT:
                eng.wait_ge(x_added, 4 * (blocks_before(FFN1, b) + 1))
            else:
                eng.wait_ge(att_added, 2 * b + h + 1)

        def kinds_before(kind, st):
            return sum(s2[0] == kind for s2 in steps[:at[st]])

        def stats_no(st):
            return sum(s2[0] in ("accT", "stats") for s2 in steps[:at[st]])

        def wait_stats_used(eng, st):
            before = [s2 for s2 in steps[:at[st]] if s2[0] in ("accT", "stats")]
            if before:
                kind, r, b = before[-1][:3]
                if kind == "stats":
                    eng.wait_ge(tok_ready, 2 * tok_writes[("norm", r, b)])
                else:
                    eng.wait_ge(x_added, 4 * (blocks_before(r, b) + 1))

        def wait_tok_idle(eng, st):
            earlier = [s2 for s2 in steps[:at[st]] if s2[0] in ("xT", "gateT") and s2[1] != ATT]
            if earlier:
                eng.wait_ge(full[ring_use[earlier[-1]][0]], ring_use[earlier[-1]][1] + 1)
            added = [s2 for s2 in steps[:at[st]] if s2[0] == "addin"]
            if added:
                eng.wait_ge(x_added, len(added))

        def xT_place(r, b):
            return place[next(st for st in place if st[:3] == ("xT", r, b))]

        def last_use(*kinds_blocks):
            return max(n for st, (ring, n) in ring_use.items() if ring == "A" and any(st[:len(k)] == k for k in kinds_blocks)) + 1

        tok_writes = {}
        for st in steps:
            if st[0] == "norm":
                tok_writes[st] = sum(k[0] == "norm" for k in tok_writes) + 1

        used_by = {v: st for st, v in ring_use.items()}
        last_c = used_by["C", c_uses_before_attention - 1]

        w2_v = w2.rearrange("e (c k) d -> e k c d", k=P)

        def normalise(eng, unit, st):
            r, b = st[1:]
            if r == ATT:
                eng.wait_ge(fold_read, 4)
            else:
                wait_tok_idle(eng, st)
            for h in range(2):
                eng.wait_ge(rstd_ready, 2 * stats_no(("stats", r, b)) + h + 1)
                for t in range(h * HT, (h + 1) * HT):
                    dst = xn[:, b * TB + t, :] if r == ATT else tok[:, t, :]
                    last = unit.tensor_scalar(dst, x[:, b * TB + t, :], mv[:, t, 0:1], rstd[:, t:t + 1], ALU.subtract, ALU.mult)
                last.then_inc(tok_ready, 1)

        block = ctx.enter_context(nc.Block())

        @block.sync
        def _(sp):
            x_v = x_in.rearrange("n (t p) d -> p (n t) d", p=P)
            out_v = out.rearrange("n (t p) d -> p (n t) d", p=P)
            att_w = [w.rearrange("d h m -> d (h m)") for w in (wq, wk, wv)]
            for h in range(2):
                sp.dma_start(x[:, h * HT:(h + 1) * HT, :], x_v[:, h * HT:(h + 1) * HT, :]).then_inc(x_loaded[h], 16)
            sp.dma_start(gw[:, :], gate_w).then_inc(small_loaded, 16)
            sp.dma_start(gb[:, :], gate_b.partition_broadcast(P)).then_inc(small_loaded, 16)
            for st in steps:
                kind, a = st[0], st[1:]
                if kind == "W":
                    u, = a
                    if u == 0:
                        continue
                    if u >= 2:
                        sp.wait_ge(w_ready, u - 1)
                    s = stage[:, u % 2, :, :]
                    if u < E:
                        sp.dma_start(s[:, 0, :], w1[u]).then_inc(stage_loaded[u % 2], 16)
                        sp.dma_start(s[:, 1, :].rearrange("k (c d) -> k c d", c=HC), w2_v[u]).then_inc(stage_loaded[u % 2], 16)
                    else:
                        for i in range(2):
                            sp.dma_start(s[:, i, :], att_w[u - E][:, i * BANK:(i + 1) * BANK]).then_inc(stage_loaded[u % 2], 16)
                    if u == 1:
                        sp.dma_start(x[:, TB:TILES, :], x_v[:, TB:TILES, :]).then_inc(x_loaded[2], 16)
                        sp.dma_start(gain[:, :], ln_g.partition_broadcast(P)).then_inc(ln_loaded, 16)
                        sp.dma_start(shift[:, :], ln_b.partition_broadcast(P)).then_inc(ln_loaded, 16)
                    if u == 8:
                        sp.dma_start(wo_sb[:, :, :], wo.rearrange("(c j) m d -> (j m) c d", j=2)).then_inc(wo_loaded, 16)
                elif kind == "kbias":
                    sp.wait_ge(full["C"], ring_use[("wvT", "C")][1] + 1)
                    sp.dma_start(bk1, bk.rearrange("h m -> (h m)").partition_broadcast(P)).then_inc(bk_loaded, 16)
                elif kind == "probsT":
                    n = place[st]
                    sp.wait_ge(pT_ready, n + 1)
                    sp.dma_start(table[n], pT[:, :]).then_inc(table_stored, 16)
                elif kind == "down" and a[2] % HC == 1:
                    r, b, s = a
                    e = s // HC
                    g = expert_no(r, b, e)
                    sp.wait_ge(table_stored, 16 * (blocks_before(r, b) + 1))
                    if (r, b, e) == (FFN2, 0, 0):
                        sp.wait_ge(out_done, NB * HP // 2)
                    if g >= 2:
                        sp.wait_ge(b_free, 2 * (g - 1))
                    row = table[blocks_before(r, b), e * TB:(e + 1) * TB, :].rearrange("t p -> (t p)")
                    sp.dma_start(pb[:, g % 2, :], row.partition_broadcast(P)).then_inc(pb_loaded[g % 2], 16)
                elif kind == "store":
                    sp.wait_ge(x_added, 4 * (blocks_before(FFN2, 0) + 1))
                    sp.dma_start(out_v[:, 0:TB, :], x[:, 0:TB, :]).then_inc(stored, 16)
                elif st == ("accT", FFN2, 1, "C"):
                    for h in range(2):
                        sp.wait_ge(x_final, h + 1)
                        tiles = slice(TB + h * HT, TB + (h + 1) * HT)
                        sp.dma_start(out_v[:, tiles, :], x[:, tiles, :]).then_inc(stored, 16)
            sp.wait_ge(stored, 48)

        @block.tensor
        def _(pe):
            def split3(o, ah, al, bh, bl, start, stop):
                nc.tensor.matmul(o, ah, bh, start=start, stop=False)
                nc.tensor.matmul(o, ah, bl, start=False, stop=False)
                return nc.tensor.matmul(o, al, bh, start=False, stop=stop)

            pe.wait_ge(ident_ready, 1)
            for _ in range(WARM_UP):
                nc.tensor.matmul(psB[:, 0, 0:P], ident[:, :], ident[:, :], start=True, stop=True)
            for st in steps:
                kind, a = st[0], st[1:]
                if st in ring_use:
                    wait_free(pe, st)
                if kind == "bias":
                    pe.wait_ge(rows_loaded, 80)
                    pe.wait_ge(ident_ready, 1)
                    nc.tensor.transpose(ps(st)[:, 0:57], rows[:, :], ident[0:57, 0:57]).then_inc(full["A"], 1)
                elif kind == "xT":
                    r, b, ring = a
                    pe.wait_ge(ident_ready, 1)
                    if r == FFN2 and b == 1:
                        pe.wait_ge(den_read, 2 * NB)
                        pe.wait_ge(oT_ready, NB)
                    for h in range(2):
                        pe.wait_ge(tok_ready, 2 * tok_writes[("norm", r, b)] - 1 + h)
                        for t in range(h * HT, (h + 1) * HT):
                            src = xn[:, b * TB + t, :] if r == ATT else tok[:, t, :]
                            last = nc.tensor.transpose(ps(st)[:, t * P:(t + 1) * P], src, ident[:, :])
                        last.then_inc(half_full if h == 0 else full[ring], 1)
                elif kind == "gate":
                    r, b, ring = a
                    pe.wait_ge(xT_ready, 2 * xT_place(r, b) + 2)
                    pe.wait_ge(gw_ready, 1)
                    for j in range(2):
                        cs = slice(j * BANK, (j + 1) * BANK)
                        nc.tensor.matmul(ps(st)[0:2 * E, cs], gw2[:, :], xh[:, b, cs], start=True, stop=False)
                        last = nc.tensor.matmul(ps(st)[0:2 * E, cs], gw2[:, :], xl[:, b, cs], start=False, stop=True)
                    last.then_inc(full[ring], 1)
                elif kind == "gateT":
                    r, b, ring = a
                    pe.wait_ge(gT_ready, place[st] + 1)
                    for t in range(TB):
                        last = nc.tensor.transpose(ps(st)[:, t * 2 * E:(t + 1) * 2 * E], gT[:, t * P:(t + 1) * P],
                                                   ident[0:2 * E, 0:2 * E])
                    last.then_inc(full[ring], 1)
                elif kind == "probsT":
                    pe.wait_ge(probs_ready, place[st] + 1)
                    nc.tensor.transpose(ps(st)[0:E * TB, 0:P], probs[:, :, :].rearrange("p e t -> p (e t)"),
                                        ident[:, :]).then_inc(full[a[2]], 1)
                elif kind == "up":
                    r, b, s = a
                    e, c = divmod(s, HC)
                    if r == FFN1 and b == 0 and c == 0:
                        if e == 0:
                            pe.wait_ge(w1_ready, 1)
                        else:
                            pe.wait_ge(w_ready, e + 1)
                    wh = Wh[:, e, 0, c * P:(c + 1) * P]
                    wl = Wl[:, e, 0, c * P:(c + 1) * P]
                    for j in range(2):
                        if s == 0:
                            pe.wait_ge(xT_ready, 2 * xT_place(r, b) + j + 1)
                        cs = slice(j * BANK, (j + 1) * BANK)
                        last = split3(ps(st)[:, cs], wh, wl, xh[:, b, cs], xl[:, b, cs], True, True)
                    last.then_inc(full["A"], 1)
                elif kind == "down":
                    r, b, s = a
                    e, c = divmod(s, HC)
                    g = expert_no(r, b, e)
                    k = blocks_before(r, b) * E * HC + s
                    if k < LAST_CHUNK:
                        pe.wait_ge(hl_ready, k + 1)
                    if k == 0:
                        pe.wait_ge(w_ready, 1)
                    if r == FFN2 and b == 0 and s == 0:
                        pe.wait_ge(kxT_ready, NB)
                    wh = Wh[:, e, 1, c * P:(c + 1) * P]
                    wl = Wl[:, e, 1, c * P:(c + 1) * P]
                    for j in range(2):
                        cs = slice(j * BANK, (j + 1) * BANK)
                        if k == LAST_CHUNK:
                            if j == 0:
                                pe.wait_ge(hl_half, 1)
                            else:
                                pe.wait_ge(hl_ready, k + 1)
                        if c == 0 and g > 0:
                            pe.wait_ge(b_free, 2 * (g - 1) + j + 1)
                        last = split3(psB[:, j, :], wh, wl, hh[:, slot(k), cs], hl[:, slot(k), cs], c == 0, c == HC - 1)
                        if c == HC - 1 and j == 0:
                            last.then_inc(b_full, 1)
                    last.then_inc(down_done, 1)
                elif kind == "accT":
                    r, b, ring = a
                    last_block = (r, b) == (FFN2, 1)
                    if not last_block:
                        pe.wait_ge(acc_added, (blocks_before(r, b) + 1) * E)
                    for h in range(2):
                        if last_block:
                            pe.wait_ge(acc_final, h + 1)
                        for t in range(h * HT, (h + 1) * HT):
                            last = nc.tensor.transpose(ps(st)[:, t * P:(t + 1) * P], acc[:, b, t * P:(t + 1) * P], ident[:, :])
                        if last_block and h == 0:
                            last.then_inc(acc_half, 1)
                    last.then_inc(full[ring], 1)
                elif kind == "bvwo":
                    pe.wait_ge(prep_ready, 1)
                    pe.wait_ge(wo_loaded, 16)
                    for c in range(HP):
                        last = nc.tensor.matmul(ps(st)[:, c * P:(c + 1) * P], kt[:, c, 0:P], wo_sb[:, c, :], start=True, stop=True)
                    last.then_inc(full["C"], 1)
                elif kind == "wvT":
                    wait_stage(pe, WU)
                    for c in range(HP):
                        wv_c = stage[:, WU % 2, :, :].rearrange("p a (c m) -> p (a c) m", m=P)[:, c, :]
                        last = nc.tensor.transpose(ps(st)[:, c * P:(c + 1) * P], wv_c, ident[:, :])
                    last.then_inc(full["C"], 1)
                elif kind == "VW":
                    hf = a[0]
                    pe.wait_ge(prep_ready, 3)
                    pe.wait_ge(fold_read, 2)
                    for q in range(HP // 2):
                        c = HP // 2 * hf + q
                        last = nc.tensor.matmul(ps(st)[:, 2 * q * P:2 * (q + 1) * P], kt[:, c, 0:P], wo2[:, c, :],
                                                start=True, stop=True)
                    last.then_inc(full["C"], 1)
                elif kind == "K":
                    n, i = a
                    if i == 0 and n % 2 == 0:
                        b = n // 2
                        pe.wait_ge(xT_ready, 2 * xT_place(ATT, b) + 2)
                        pe.wait_ge(w_ready, WU)
                        pe.wait_ge(consts_ready, 1)
                    ts_ = slice((ST * (n % 2) + i) * P, (ST * (n % 2) + i + 1) * P)
                    for j in range(2):
                        cs = slice(j * BANK, (j + 1) * BANK)
                        last = split3(ps(st)[:, cs], xh[:, n // 2, ts_], xl[:, n // 2, ts_], Ah[:, 1, cs], Al[:, 1, cs], True, True)
                    last.then_inc(full["A"], 1)
                elif kind == "Q":
                    n, j = a
                    cs = slice((n % 2) * BANK, (n % 2 + 1) * BANK)
                    for q in range(2):
                        c = 2 * j + q
                        last = split3(ps(st)[:, q * BANK:(q + 1) * BANK], Ah[:, 0, c * P:(c + 1) * P], Al[:, 0, c * P:(c + 1) * P],
                                      xh[:, n // 2, cs], xl[:, n // 2, cs], True, True)
                    last.then_inc(full["A"], 1)
                elif kind == "kv":
                    n, i = a
                    ti = ST * n + i
                    pe.wait_ge(feature_ready, feature_use[("K", n, i)] + 1)
                    if i == 0 and n == 0:
                        pe.wait_ge(b_free, 2 * 2 * E)
                    if i == 0 and n > 0:
                        pe.wait_ge(kxT_ready, n)
                    for j in range(2):
                        last = nc.tensor.matmul(psB[:, j, :], xn[:, ti, :], km[:, ti % 2, j * BANK:(j + 1) * BANK],
                                                start=(i == 0), stop=(i == ST - 1))
                    last.then_inc(kv_done, 1)
                elif kind == "ksum":
                    n, = a
                    pe.wait_ge(kt_added, (ST - 1) * (n + 1))
                    if n == 0:
                        wait_left(pe, last_c)
                    for c in range(HP):
                        last = nc.tensor.matmul(ksum_ps[:, c:c + 1], kt[:, c, :], ones[:, :], start=True, stop=True)
                    last.then_inc(ksum_full, 1)
                elif kind == "G":
                    n, = a
                    pe.wait_ge(kxT_ready, n + 1)
                    for h in range(2 * HP):
                        c, j = divmod(h, 2)
                        hs = slice(64 * j, 64 * j + 64)
                        last = nc.tensor.matmul(ps(st)[hs, c * P:(c + 1) * P], kxT[:, c, hs], VW[:, c, j * P:(j + 1) * P],
                                                start=True, stop=True)
                    last.then_inc(full["A"], 1)
                elif kind == "den":
                    n, hf = a
                    pe.wait_ge(ksum_ready, n + 1)
                    pe.wait_ge(feature_ready, feature_use[("Q", n, 3)] + 1)
                    if hf == 1 and n > 0:
                        pe.wait_ge(oT_ready, n)
                    for c in range(HP):
                        last = nc.tensor.matmul(den_ps(hf), ksum[:, 16 * c:16 * (c + 1)],
                                                qm[:, c, hf * BANK // 2:(hf + 1) * BANK // 2],
                                                start=(c == 0), stop=(c == HP - 1))
                    last.then_inc(den_full, 1)
                elif kind == "z":
                    n, j = a
                    pe.wait_ge(z_ready, n + 1)
                    for q in range(2):
                        c = 2 * j + q
                        last = nc.tensor.matmul(ps(st)[:, q * BANK:(q + 1) * BANK], pick[:, c, :], z2[:, :], start=True, stop=True)
                    last.then_inc(full["A"], 1)
                elif kind == "out":
                    n, j = a
                    pe.wait_ge(qz_ready, HP // 2 * n + j + 1)
                    pe.wait_ge(G_ready, n + 1)
                    if j == 0:
                        pe.wait_ge(den_read, 2 * (n + 1))
                    for c in (2 * j, 2 * j + 1):
                        last = nc.tensor.matmul(psC[:, 1, :], Gs[:, c, :], qm[:, c, :], start=(c == 0), stop=(c == HP - 1))
                    last.then_inc(out_done, 1)
                elif kind == "oT":
                    n, = a
                    pe.wait_ge(oT_ready, n + 1)
                    for t in range(ST):
                        last = nc.tensor.transpose(ps(st)[:, t * P:(t + 1) * P], oT[:, t * P:(t + 1) * P], ident[:, :])
                    last.then_inc(full["A"], 1)

        @block.scalar
        def _(act):
            act.dma_start(stage[:, 0, 0, :], w1[0]).then_inc(w1_loaded, 16)
            act.dma_start(stage[:, 0, 1, :].rearrange("k (c d) -> k c d", c=HC), w2_v[0]).then_inc(w2_loaded, 16)
            act.wait_ge(ident_ready, 1)
            nc.scalar.activation(warm[:, :], half[:, 0:1], ACT.Gelu)
            act.dma_start(rows[0:32, :], b1.rearrange("e (c k) -> (e c) k", k=P)).then_inc(rows_loaded, 16)
            act.dma_start(rows[32:40, :], b2).then_inc(rows_loaded, 16)
            act.dma_start(rows[40:48, :], bq.rearrange("(c j) m -> c (j m)", j=2)).then_inc(rows_loaded, 16)
            act.dma_start(rows[48:56, :], bv.rearrange("(c j) m -> c (j m)", j=2)).then_inc(rows_loaded, 16)
            act.dma_start(rows[56:57, :], bo.rearrange("(a d) -> a d", a=1)).then_inc(rows_loaded, 16)
            for st in steps:
                kind, a = st[0], st[1:]
                if kind == "W0":
                    act.wait_ge((w1_loaded, w2_loaded)[a[0]], 16)
                    nc.scalar.copy(Wh[:, 0, a[0], :], stage[:, 0, a[0], :]).then_inc(hi_split, 1)
                elif kind == "bias":
                    wait_full(act, st)
                    nc.scalar.copy(cols[:, :], ps(st)[:, 0:57]).then_inc(cols_ready, 1)
                elif kind == "xT":
                    r, b, ring = a
                    if r == ATT:
                        act.wait_ge(full["A"], last_use(("up", FFN1, b)))
                    if r == FFN2:
                        m = 2 * b + 1
                        act.wait_ge(full["A"], last_use(("K", m), ("Q", m)))
                    for h in range(2):
                        if h == 0:
                            act.wait_ge(half_full, place[st] + 1)
                        else:
                            wait_full(act, st)
                        cs = slice(h * BANK, (h + 1) * BANK)
                        nc.scalar.copy(xh[:, b, cs], ps(st)[:, cs]).then_inc(xh_ready, 1)
                elif kind == "gate":
                    wait_full(act, st)
                    nc.scalar.copy(gT, ps(st)[0:2 * E, :]).then_inc(gT_ready, 1)
                elif kind == "up":
                    r, b, s = a
                    k = blocks_before(r, b) * E * HC + s
                    if k == 0:
                        act.wait_ge(cols_ready, 1)
                    if r == FFN2 and b == 0 and s == 0:
                        act.wait_ge(feature_ready, len(feature_use))
                        act.wait_ge(kv_done, NB * ST)
                        act.wait_ge(kt_added, NB * (ST - 1))
                    wait_full(act, st)
                    if k >= HS:
                        act.wait_ge(down_done, k - HS + 1)
                    if k >= 2:
                        act.wait_ge(hl_ready, k - 1)
                    bias = cols[:, s:s + 1]
                    if k < LAST_CHUNK:
                        nc.scalar.activation(hh[:, slot(k), :], ps(st), ACT.Gelu, bias=bias)
                        nc.scalar.activation(hid[:, k % 2, :], ps(st), ACT.Gelu, bias=bias).then_inc(hid_ready, 1)
                    else:
                        for h in range(2):
                            cs = slice(h * BANK, (h + 1) * BANK)
                            nc.scalar.activation(hh[:, slot(k), cs], ps(st)[:, cs], ACT.Gelu, bias=bias)
                            nc.scalar.activation(hid[:, k % 2, cs], ps(st)[:, cs], ACT.Gelu, bias=bias)\
                                .then_inc(hid_ready if h else hid_half, 1)
                elif kind == "accT" and a[0:2] != (FFN2, 1):
                    r, b, ring = a
                    wait_full(act, st)
                    wait_tok_idle(act, st)
                    nc.scalar.copy(tok[:, :, :].rearrange("p t d -> p (t d)"), ps(st)).then_inc(acc_in_tok, 1)
                elif kind == "K":
                    n, i = a
                    k = feature_use[st]
                    act.wait_ge(R_ready, ST * n + i + 1)
                    if k == 0:
                        act.wait_ge(hl_ready, 2 * E * HC - 1)
                    if k == 1:
                        act.wait_ge(down_done, 2 * E * HC)
                    if k >= 2:
                        act.wait_ge(feature_ready, k - 1)
                    nc.scalar.activation(X[:, fslot(k), :], R[:, fslot(k), :], ACT.Exp, bias=less1[:, :]).then_inc(X_ready, 1)
                elif kind == "Q":
                    n, j = a
                    k = feature_use[st]
                    wait_full(act, st)
                    act.wait_ge(feature_ready, k - 1)
                    for q in range(2):
                        cs = slice(q * BANK, (q + 1) * BANK)
                        bias = cols[:, 40 + 2 * j + q:41 + 2 * j + q]
                        nc.scalar.activation(X[:, fslot(k), cs], ps(st)[:, cs], ACT.Exp, bias=bias)
                        last = nc.scalar.activation(R[:, fslot(k), cs], ps(st)[:, cs], ACT.Relu, bias=bias)
                    last.then_inc(X_ready, 1)
                elif kind in ("bvwo", "wvT", "VW"):
                    wait_full(act, st)
                    if kind == "bvwo":
                        act.wait_ge(w_ready, WU)
                    dst = {"bvwo": bvwo, "wvT": kt[:, :, 0:P], "VW": VW[:, HP // 2 * place[st]:HP // 2 * (place[st] + 1), :]}[kind]
                    m = 2 * P if kind == "VW" else P
                    nc.scalar.copy(dst, ps(st).rearrange("p (c m) -> p c m", m=m)).then_inc(fold_read, 1)
                elif kind == "kvout":
                    n, = a
                    act.wait_ge(kv_done, ST * (n + 1))
                    if n == 0:
                        act.wait_ge(b_free, 2 * 2 * E)
                    else:
                        act.wait_ge(full["A"], ring_use[("G", n - 1)][1] + 1)
                    nc.scalar.copy(kxT[:, :, :].rearrange("p c m -> p (c m)"), psB[:, :, :].rearrange("p a n -> p (a n)"))\
                        .then_inc(kxT_ready, 1)
                elif kind == "ksum":
                    n, = a
                    act.wait_ge(ksum_full, n + 1)
                    if n > 0:
                        act.wait_ge(den_full, 2 * n)
                        act.wait_ge(bias_ready, n)
                    nc.scalar.copy(kcol[:, :], ksum_ps)
                    for j in range(2):
                        hs = slice(64 * j, 64 * j + 64)
                        last = nc.scalar.copy(ksum[hs, j:j + 18 * HP - 17:18], ksum_ps[hs, :])
                    last.then_inc(ksum_ready, 1)
                elif kind == "outc":
                    n, = a
                    act.wait_ge(out_done, HP // 2 * (n + 1))
                    if n > 0:
                        act.wait_ge(full["A"], ring_use[("oT", n - 1)][1] + 1)
                    nc.scalar.activation(oT[:, :], psC[:, 1, :], ACT.Identity, bias=cols[:, 56:57]).then_inc(oT_ready, 1)

        @block.vector
        def _(dve):
            link_count = [0]

            def link(ins):
                link_count[0] += 1
                ins.then_inc(dve_chain, 1)
                dve.wait_ge(dve_chain, link_count[0])

            def half_stats(h, src):
                for t in range(h * HT, (h + 1) * HT):
                    last = nc.vector.bn_stats(bst[:, t, :], src(t))
                link(last)
                for t in range(h * HT, (h + 1) * HT):
                    last = nc.vector.bn_aggr(mv[:, t, :], bst[:, t, :])
                last.then_inc(stats_ready, 1)

            def bc(v):
                return v.unsqueeze(2).to_broadcast([P, TB, E])

            for st in steps:
                kind, a = st[0], st[1:]
                if kind == "W" and a[0] == 0:
                    nc.vector.memset(z2[:, :].bitcast(F32), 0.0)
                elif kind == "stats":
                    r, b = a
                    wait_stats_used(dve, st)
                    wait_x(dve, r, b, 0)
                    half_stats(0, lambda t: x[:, b * TB + t, :])
                elif kind == "stats2":
                    r, b = a[0:2]
                    if len(a) == 2:
                        wait_x(dve, r, b, 1)
                        half_stats(1, lambda t: x[:, b * TB + t, :])
                    else:
                        half_stats(1, lambda t: tok[:, t, :])
                elif kind == "W0":
                    dve.wait_ge(hi_split, a[0] + 1)
                    nc.vector.tensor_tensor(Wl[:, 0, a[0], :], stage[:, 0, a[0], :], Wh[:, 0, a[0], :].bitcast(F32),
                                            ALU.subtract).then_inc(w_ready if a[0] else w1_ready, 1)
                elif kind == "bias":
                    dve.wait_ge(small_loaded, 32)
                    link(nc.vector.tensor_copy(gw2[:, 0:E], gw[:, :]))
                    nc.vector.tensor_tensor(gw2[:, E:2 * E], gw[:, :], gw2[:, 0:E].bitcast(F32), ALU.subtract)\
                        .then_inc(gw_ready, 1)
                elif kind == "norm" and tuple(a) in NORMS_OF_DVE:
                    normalise(dve, nc.vector, st)
                elif kind == "xT":
                    r, b, ring = a
                    for h in range(2):
                        dve.wait_ge(xh_ready, 2 * place[st] + h + 1)
                        cs = slice(h * BANK, (h + 1) * BANK)
                        nc.vector.tensor_tensor(xl[:, b, cs], ps(st)[:, cs], xh[:, b, cs].bitcast(F32), ALU.subtract)\
                            .then_inc(xT_ready, 1)
                elif kind == "gateT":
                    wait_full(dve, st)
                    parts = ps(st)[:, 0:TB * 2 * E].rearrange("p (t u e) -> p t u e", t=TB, u=2)
                    link(nc.vector.tensor_tensor(gL[:, :, :], parts[:, :, 1, :], gb[:, :].unsqueeze(1).to_broadcast([P, TB, E]),
                                                 ALU.add))
                    nc.vector.tensor_tensor(gL[:, :, :], parts[:, :, 0, :], gL[:, :, :], ALU.add).then_inc(logits_read, 1)
                    dve.wait_ge(logits_read, place[st] + 1)
                    link(nc.vector.tensor_reduce(gm1[:, :], gL[:, :, :], AX_X, ALU.max))
                elif kind == "rank":
                    i = a[2]
                    rank = order[:, :].unsqueeze(1).to_broadcast([P, TB, E])
                    if i == 0:
                        link(nc.vector.tensor_tensor(gA[:, :, :], gL[:, :, :], bc(gm1[:, :]), ALU.is_equal))
                        link(nc.vector.tensor_tensor(gA[:, :, :], gA[:, :, :], rank, ALU.mult))
                        link(nc.vector.tensor_reduce(gm2[:, :], gA[:, :, :], AX_X, ALU.max))
                    elif i == 1:
                        link(nc.vector.tensor_tensor(gS[:, :, :], gA[:, :, :], bc(gm2[:, :]), ALU.is_equal))
                        link(nc.vector.scalar_tensor_tensor(gX[:, :, :], gS[:, :, :], FAR, gL[:, :, :], ALU.mult, ALU.add))
                        link(nc.vector.tensor_reduce(gm2[:, :], gX[:, :, :], AX_X, ALU.max))
                        nc.vector.tensor_tensor(g2nd[:, :], gm2[:, :], gm1[:, :], ALU.subtract).then_inc(logits_ready, 1)
                    elif i == 2:
                        link(nc.vector.tensor_tensor(gA[:, :, :], gX[:, :, :], bc(gm2[:, :]), ALU.is_equal))
                        link(nc.vector.tensor_tensor(gA[:, :, :], gA[:, :, :], rank, ALU.mult))
                        link(nc.vector.tensor_reduce(gm2[:, :], gA[:, :, :], AX_X, ALU.max))
                    else:
                        link(nc.vector.tensor_tensor(gA[:, :, :], gA[:, :, :], bc(gm2[:, :]), ALU.is_equal))
                elif kind == "probs":
                    dve.wait_ge(exp_ready, place[st] + 1)
                    link(nc.vector.tensor_scalar(gsum[:, :], g2nd[:, :], 1.0, None, ALU.add))
                    link(nc.vector.reciprocal(gsum[:, :], gsum[:, :]))
                    link(nc.vector.tensor_tensor(gm2[:, :], g2nd[:, :], gsum[:, :], ALU.mult))
                    nc.vector.tensor_tensor(gS[:, :, :], gS[:, :, :], bc(gsum[:, :]), ALU.mult)
                    link(nc.vector.tensor_tensor(gA[:, :, :], gA[:, :, :], bc(gm2[:, :]), ALU.mult))
                    nc.vector.tensor_tensor(probs[:, :, :].rearrange("p e t -> p t e"), gS[:, :, :], gA[:, :, :], ALU.add)\
                        .then_inc(probs_ready, 1)
                elif kind == "probsT":
                    wait_full(dve, st)
                    if place[st]:
                        dve.wait_ge(table_stored, 16 * place[st])
                    nc.vector.tensor_copy(pT[:, :], ps(st)[0:E * TB, 0:P]).then_inc(pT_ready, 1)
                elif kind == "low":
                    r, b, s = a
                    k = blocks_before(r, b) * E * HC + s
                    if k == LAST_CHUNK:
                        dve.wait_ge(hid_half, 1)
                        dve.wait_ge(down_done, k - HS + 1)
                        cs = slice(0, BANK)
                        nc.vector.tensor_tensor(hl[:, slot(k), cs], hid[:, k % 2, cs], hh[:, slot(k), cs].bitcast(F32),
                                                ALU.subtract).then_inc(hl_half, 1)
                    dve.wait_ge(hid_ready, k + 1)
                    if k >= HS:
                        dve.wait_ge(down_done, k - HS + 1)
                    if r == FFN2 and b == 0 and s < HS:
                        dve.wait_ge(kv_done, NB * ST)
                        dve.wait_ge(kt_added, NB * (ST - 1))
                        if s:
                            dve.wait_ge(out_done, (NB - 1) * HP // 2 + s)
                    cs = slice(BANK if k == LAST_CHUNK else 0, 2 * BANK)
                    nc.vector.tensor_tensor(hl[:, slot(k), cs], hid[:, k % 2, cs], hh[:, slot(k), cs].bitcast(F32),
                                            ALU.subtract).then_inc(hl_ready, 1)
                elif kind == "down" and a[2] % HC == HC - 1:
                    r, b, s = a
                    e = s // HC
                    g = expert_no(r, b, e)
                    k = blocks_before(r, b) * E * HC + s
                    dve.wait_ge(pb_loaded[g % 2], 16 * (g // 2 + 1))
                    if e == 0 and (r, b) != (FFN1, 0) and (r, b) != (FFN1, 1):
                        pr = ("accT", FFN1, b, "A" if b else "C")
                        dve.wait_ge(full[pr[3]], ring_use[pr][1] + 1)
                    if (r, b, e) == (FFN2, 0, 0):
                        dve.wait_ge(out_done, NB * HP // 2)
                    if g >= 2:
                        dve.wait_ge(acc_added, g - 1)
                    for j in range(2):
                        cs = slice(j * BANK, (j + 1) * BANK)
                        if j == 0:
                            dve.wait_ge(b_full, g + 1)
                        else:
                            dve.wait_ge(down_done, k + 1)
                        dst = acc[:, b, cs] if e == 0 else gated[:, g % 2, cs]
                        last = nc.vector.scalar_tensor_tensor(dst, psB[:, j, :], cols[:, 32 + e:33 + e], pb[:, g % 2, cs],
                                                              ALU.add, ALU.mult)
                        last.then_inc(b_free, 1)
                        if (r, b, e) == (FFN2, 1, E - 1):
                            if j == 0:
                                dve.wait_ge(acc_added, g)
                            dve.wait_ge(b_free, 2 * g + j + 1)
                            nc.vector.tensor_tensor(acc[:, b, cs], acc[:, b, cs], gated[:, g % 2, cs], ALU.add).then_inc(acc_final, 1)
                elif kind == "accT":
                    r, b, ring = a
                    wait_stats_used(dve, st)
                    if (r, b) != (FFN2, 1):
                        dve.wait_ge(acc_in_tok, place[st] + 1)
                        half_stats(0, lambda t: tok[:, t, :])
                        continue
                    wait_tok_idle(dve, st)
                    n = stats_no(st)

                    def finish(h):
                        dve.wait_ge(rstd_ready, 2 * n + h + 1)
                        for t in range(h * HT, (h + 1) * HT):
                            xt = x[:, b * TB + t, :]
                            last = nc.vector.scalar_tensor_tensor(xt, tok[:, t, :], rstd[:, t:t + 1], xt, ALU.mult, ALU.add)
                        last.then_inc(x_final, 1)

                    dve.wait_ge(x_shifted, 2 * 2)
                    for h in range(2):
                        if h == 0:
                            dve.wait_ge(acc_half, 1)
                        else:
                            wait_full(dve, st)
                        half_stats(h, lambda t: ps(st)[:, t * P:(t + 1) * P])
                        if h == 1:
                            finish(0)
                        dve.wait_ge(stats_ready, 2 * n + h + 1)
                        for t in range(h * HT, (h + 1) * HT):
                            last = nc.vector.scalar_tensor_tensor(tok[:, t, :], ps(st)[:, t * P:(t + 1) * P], mv[:, t, 0:1],
                                                                  gain[:, :], ALU.subtract, ALU.mult)
                        link(last)
                    finish(1)
                elif kind == "K":
                    n, i = a
                    k = feature_use[st]
                    wait_full(dve, st)
                    if k < 2:
                        dve.wait_ge(down_done, 2 * E * HC - 1 - k)
                        dve.wait_ge(bk1_ready, 1)
                    if k >= 2:
                        dve.wait_ge(feature_ready, k - 1)
                    nc.vector.tensor_tensor(R[:, fslot(k), :], ps(st), bk1, ALU.add).then_inc(R_ready, 1)
                elif kind == "G":
                    n, = a
                    wait_full(dve, st)
                    dve.wait_ge(bias_ready, n + 1)
                    Gf = Gs[:, :, :].rearrange("p c m -> p (c m)")
                    nc.vector.tensor_tensor(Gf, ps(st), Gf, ALU.add).then_inc(G_ready, 1)
                elif kind in ("Kf", "Qf"):
                    n, i = a
                    k = feature_use[(kind[0], n, i)]
                    dve.wait_ge(X_ready, k + 1)
                    if kind == "Kf":
                        ti = ST * n + i
                        if ti == 0:
                            dve.wait_ge(hl_ready, 2 * E * HC)
                        if ti == 1:
                            dve.wait_ge(down_done, 2 * E * HC - 2)
                        if ti >= 2:
                            dve.wait_ge(kv_done, ti - 1)
                            dve.wait_ge(kt_added, adds_of(ti - 2))
                        dst = km[:, ti % 2, :]
                    else:
                        if n == 0 and i < 2:
                            dve.wait_ge(down_done, 2 * E * HC - 1 + i)
                        if n == 0 and i == 2:
                            dve.wait_ge(acc_added, 2 * E)
                        if n > 0:
                            dve.wait_ge(out_done, HP // 2 * (n - 1) + i + 1)
                        dst = qm[:, 2 * i:2 * i + 2, :].rearrange("p c n -> p (c n)")
                    nc.vector.scalar_tensor_tensor(dst, X[:, fslot(k), :], 1.0, R[:, fslot(k), :], ALU.min,
                                                   ALU.max if kind == "Kf" else ALU.add)\
                        .then_inc(feature_ready, 1)
                elif kind == "denz":
                    n, hf = a
                    if hf == 0 and n > 0:
                        dve.wait_ge(full["A"], ring_use[("oT", n - 1)][1] + 1)
                    dve.wait_ge(den_full, 2 * n + hf + 1)
                    cs = slice(hf * BANK // 2, (hf + 1) * BANK // 2)
                    nc.vector.tensor_scalar(zr[:, cs], den_ps(hf), ATT_EPS, None, ALU.add).then_inc(den_read, 1)
                    dve.wait_ge(den_read, 2 * n + hf + 1)
                    link(nc.vector.reciprocal(zr[:, cs], zr[:, cs]))
                    if hf == 0 and n > 0:
                        dve.wait_ge(full["A"], ring_use[("z", n - 1, 3)][1] + 1)
                    link(nc.vector.tensor_copy(z2[0:16, cs], zr[:, cs]))
                    last = nc.vector.tensor_tensor(z2[32:48, cs], zr[:, cs], z2[0:16, cs].bitcast(F32), ALU.subtract)
                    if hf == 1:
                        last.then_inc(z_ready, 1)
                elif kind == "z":
                    n, j = a
                    wait_full(dve, st)
                    q2 = qm[:, 2 * j:2 * j + 2, :].rearrange("p c n -> p (c n)")
                    nc.vector.tensor_tensor(q2, q2, ps(st), ALU.mult).then_inc(qz_ready, 1)
                elif kind == "oT":
                    n, = a
                    wait_full(dve, st)
                    xb = x[:, ST * n:ST * (n + 1), :]
                    nc.vector.tensor_tensor(xb, xb, ps(st)[:, 0:BANK].rearrange("p (t d) -> p t d", t=ST),
                                            ALU.add).then_inc(att_added, 1)

        @block.gpsimd
        def _(pool):
            link_count = [0]

            def link(ins):
                link_count[0] += 1
                ins.then_inc(pool_chain, 1)
                pool.wait_ge(pool_chain, link_count[0])

            link(nc.gpsimd.memset(ident[:, :], 0.0))
            nc.gpsimd.affine_select(out=ident[:, :], in_=ident[:, :], compare_op=ALU.not_equal, fill=1.0, base=0,
                                    pattern=[[-1, P]], channel_multiplier=1)
            for e in range(E):
                nc.gpsimd.memset(order[:, e:e + 1], float(E - e))
            nc.gpsimd.memset(two[:, :], 2.0)
            nc.gpsimd.memset(less1[:, :], -1.0)
            link(nc.gpsimd.memset(half[:, :], -0.5))
            pool.engine_nop().then_inc(ident_ready, 1)
            for st in steps:
                kind, a = st[0], st[1:]
                if kind in ("stats", "accT"):
                    wait_stats_used(pool, st)
                    for h in range(2):
                        ts_ = slice(h * HT, (h + 1) * HT)
                        pool.wait_ge(stats_ready, 2 * stats_no(st) + h + 1)
                        link(nc.gpsimd.tensor_scalar(ve[:, ts_], mv[:, ts_, 1], LN_EPS, 1.0, ALU.add, ALU.mult))
                        nc.gpsimd.tensor_tensor(rstd[:, ts_], ve[:, ts_], half[:, ts_], ALU.pow).then_inc(rstd_ready, 1)
                    if kind == "stats" and st[1:] == (FFN1, 0):
                        pool.wait_ge(ln_loaded, 32)
                        link(nc.gpsimd.tensor_scalar(gain[:, :], gain[:, :], 0.5, 1.0, ALU.mult, ALU.mult))
                        link(nc.gpsimd.tensor_scalar(shift[:, :], shift[:, :], 0.5, 1.0, ALU.mult, ALU.mult))
                if kind == "rank" and a[2] == 1:
                    n = kinds_before("rank", st) // 4
                    pool.wait_ge(logits_ready, n + 1)
                    link(nc.gpsimd.tensor_scalar(g2nd[:, :], g2nd[:, :], LOG2_E, 1.0 / TEMP, ALU.mult, ALU.mult))
                    nc.gpsimd.tensor_tensor(g2nd[:, :], two[:, :], g2nd[:, :], ALU.pow).then_inc(exp_ready, 1)
                elif kind == "consts":
                    flat = kt[0:48, :, :].rearrange("k c m -> k (c m)")
                    link(nc.gpsimd.memset(flat, 0.0))
                    v = kt[0:48, :, :].rearrange("k c (j m) -> k c j m", j=2)
                    for row in (0, 32):
                        link(nc.gpsimd.affine_select(out=v, in_=v, compare_op=ALU.not_equal, fill=1.0, base=-row,
                                                     pattern=[[-2, HP], [-1, 2], [0, P // 2]], channel_multiplier=1))
                    link(nc.gpsimd.tensor_scalar(pick[:, :, :].rearrange("k c m -> k (c m)"), flat, 1.0, 1.0, ALU.mult, ALU.mult))
                    nc.gpsimd.memset(ones[:, :], 1.0)
                    nc.gpsimd.memset(ksum[:, :], 0.0).then_inc(consts_ready, 1)
                elif kind == "prep":
                    heads = [slice(0, 64), slice(64, P)]
                    if a[0] == 0:
                        link(nc.gpsimd.memset(kt[:, :, :], 0.0))
                        for hs in heads:
                            link(nc.gpsimd.tensor_copy(kt[hs, :, hs], cols[hs, 48:56].unsqueeze(2).to_broadcast([64, HP, 64])))
                    else:
                        if a[0] == 1:
                            pool.wait_ge(wo_loaded, 16)
                            link(nc.gpsimd.memset(wo2, 0.0))
                        j = a[0] - 1
                        link(nc.gpsimd.tensor_copy(wo2[heads[j], :, j * P:(j + 1) * P], wo_sb[heads[j], :, :]))
                    pool.engine_nop().then_inc(prep_ready, 1)
                elif st == ("VW", 1, "C"):
                    pool.wait_ge(bk_loaded, 16)
                    nc.gpsimd.tensor_scalar(bk1, bk1, 1.0, 1.0, ALU.add, ALU.mult).then_inc(bk1_ready, 1)
                elif kind == "Kf" and a[1] > 0:
                    n, i = a
                    pool.wait_ge(feature_ready, feature_use[("K", n, i)] + 1)
                    ktf = kt[:, :, :].rearrange("p c m -> p (c m)")
                    if i == 1:
                        if n == 0:
                            pool.wait_ge(fold_read, 4)
                        else:
                            pool.wait_ge(ksum_full, n)
                        first = km[:, (ST * n) % 2, :]
                    else:
                        pool.wait_ge(kt_added, (ST - 1) * n + i - 1)
                        first = ktf
                    nc.gpsimd.tensor_tensor(ktf, first, km[:, (ST * n + i) % 2, :], ALU.add).then_inc(kt_added, 1)
                elif kind == "ksum":
                    n, = a
                    pool.wait_ge(ksum_ready, n + 1)
                    if n > 0:
                        pool.wait_ge(out_done, HP // 2 * n)
                    else:
                        pool.wait_ge(b_free, 2 * 2 * E)
                    nc.gpsimd.tensor_tensor(Gs[:, :, :], bvwo, kcol[:, :].unsqueeze(2).to_broadcast([P, HP, P]), ALU.mult)\
                        .then_inc(bias_ready, 1)
                elif kind == "W" and 0 < a[0] < WU:
                    u, = a
                    wait_stage(pool, u)
                    s = stage[:, u % 2, :, :]
                    h, l = (Wh[:, u, :, :], Wl[:, u, :, :]) if u < E else (
                        Ah[:, u - E, :].rearrange("p (a n) -> p a n", a=2), Al[:, u - E, :].rearrange("p (a n) -> p a n", a=2))
                    link(nc.gpsimd.tensor_scalar(h, s, 1.0, 1.0, ALU.mult, ALU.mult))
                    if u == 1:
                        pool.wait_ge(w_ready, 1)
                    nc.gpsimd.tensor_tensor(l, s, h.bitcast(F32), ALU.subtract).then_inc(w_ready, 1)
                elif kind == "addin":
                    r, b, q = a
                    pool.wait_ge(rstd_ready, 2 * stats_no(next(s2 for s2 in steps if s2[:3] == ("accT", r, b))) + 2)
                    tiles = slice(TB // 4 * q, TB // 4 * (q + 1))
                    for t in range(tiles.start, tiles.stop):
                        last = nc.gpsimd.tensor_scalar(tok[:, t, :], tok[:, t, :], mv[:, t, 0:1], rstd[:, t:t + 1],
                                                       ALU.subtract, ALU.mult)
                    link(last)
                    link(nc.gpsimd.tensor_tensor(tok[:, tiles, :], tok[:, tiles, :],
                                                 gain[:, :].unsqueeze(1).to_broadcast([P, TB // 4, P]), ALU.mult))
                    xb = x[:, b * TB + tiles.start:b * TB + tiles.stop, :]
                    nc.gpsimd.tensor_tensor(xb, xb, tok[:, tiles, :], ALU.add).then_inc(x_added, 1)
                if kind == "norm":
                    r, b = a
                    if (r, b) not in NORMS_OF_DVE:
                        normalise(pool, nc.gpsimd, st)
                    if r == ATT:
                        continue
                    pool.wait_ge(tok_ready, 2 * tok_writes[st])
                    xb = x[:, b * TB:(b + 1) * TB, :]
                    nc.gpsimd.tensor_tensor(xb, xb, shift[:, :].unsqueeze(1).to_broadcast([P, TB, P]), ALU.add)\
                        .then_inc(x_shifted, 1)
                elif kind == "down" and a[2] % HC == HC - 1:
                    r, b, s = a
                    e = s // HC
                    g = expert_no(r, b, e)
                    if (r, b, e) == (FFN2, 1, E - 1):
                        continue
                    pool.wait_ge(b_free, 2 * (g + 1))
                    if g:
                        pool.wait_ge(acc_added, g)
                    if e == 0:
                        pool.engine_nop().then_inc(acc_added, 1)
                    else:
                        nc.gpsimd.tensor_tensor(acc[:, b, :], acc[:, b, :], gated[:, g % 2, :], ALU.add).then_inc(acc_added, 1)


_INS = ['L0_attn_x', 'L0_attn_wq', 'L0_attn_bq', 'L0_attn_wk', 'L0_attn_bk', 'L0_attn_wv', 'L0_attn_bv', 'L0_attn_wo',
        'L0_attn_bo', 'L0_ffn_gate_w', 'L0_ffn_gate_b', 'L0_ffn_w1', 'L0_ffn_b1', 'L0_ffn_w2', 'L0_ffn_b2',
        'L0_ffn_ln_g', 'L0_ffn_ln_b']
_OUTS = [((4, 512, 128), 'float32')]


def kernel(**inputs):
    import numpy as _np
    import concourse.bacc as _bacc
    from concourse import mybir as _mybir
    from concourse.bass_utils import run_bass_kernel_spmd as _run

    nc = _bacc.Bacc("TRN2", target_bir_lowering=False, num_devices=1)
    arrays, args = {}, []
    for name in _INS:
        a = _np.ascontiguousarray(inputs[name])
        arrays[f"in_{name}_dram"] = a
        args.append(nc.dram_tensor(f"in_{name}_dram", a.shape, _mybir.dt.from_np(a.dtype), kind="ExternalInput").ap())
    for i, (shape, dtype) in enumerate(_OUTS):
        dt = _mybir.dt.from_np(_np.dtype(dtype))
        args.append(nc.dram_tensor(f"out_{i}_dram", shape, dt, kind="ExternalOutput").ap())
    bass_macaron_kernel(nc, *args)
    r = _run(nc, [arrays], core_ids=[0])
    got = tuple(r.results[0][f"out_{i}_dram"] for i in range(len(_OUTS)))
    return got[0]
```
